# Optimizing a Trainium2 kernel written in Bass

```python
import numpy as np
import jax
import jax.numpy as jnp

def _softmax(x, axis=-1):
    return jax.nn.softmax(x, axis=axis)

def _gelu(x):
    return jax.nn.gelu(x, approximate=True)

def _silu(x):
    return jax.nn.silu(x)

def _sigmoid(x):
    return jax.nn.sigmoid(x)

def _layernorm(x, axis=-1, eps=1e-05):
    m = jnp.mean(x, axis=axis, keepdims=True)
    v = jnp.var(x, axis=axis, keepdims=True)
    return (x - m) / jnp.sqrt(v + eps)

def _scatter_add(tgt, idx, src, axis=0):
    return tgt.at[idx].add(src)

def _segment_sum(src, seg, n):
    return jax.ops.segment_sum(src, seg, n)
kernel_name = 'mk_seq_postln_d1_jaxref_r8_5fa99a'

def setup_inputs(seed: int=0):
    np.random.seed(seed)
    _w = jnp.asarray

    def _L0_attn_setup():
        import jax, jax.numpy as jnp
        import numpy as np
        from jax import lax
        D_MODEL, D_STATE, D_CONV, EXPAND = (128, 16, 4, 2)
        D_INNER = EXPAND * D_MODEL
        B, L = (2, 256)
        key = jax.random.key(seed)
        ks = jax.random.split(key, 8)
        s_in = 1.0 / np.sqrt(D_MODEL)
        s_xp = 1.0 / np.sqrt(D_INNER)
        x = jax.random.normal(ks[0], (B, L, D_MODEL), dtype=jnp.float32)
        W_in = jax.random.uniform(ks[1], (2 * D_INNER, D_MODEL), minval=-s_in, maxval=s_in)
        conv_w = jax.random.uniform(ks[2], (D_INNER, 1, D_CONV), minval=-0.5, maxval=0.5)
        conv_b = jax.random.uniform(ks[3], (D_INNER,), minval=-0.5, maxval=0.5)
        W_xproj = jax.random.uniform(ks[4], (1 + 2 * D_STATE, D_INNER), minval=-s_xp, maxval=s_xp)
        W_dt = jax.random.uniform(ks[5], (D_INNER, 1), minval=-1.0, maxval=1.0)
        b_dt = jax.random.uniform(ks[6], (D_INNER,), minval=-1.0, maxval=1.0)
        A_log = jnp.log(jnp.broadcast_to(jnp.arange(1, D_STATE + 1, dtype=jnp.float32), (D_INNER, D_STATE)))
        D = jnp.ones((D_INNER,), dtype=jnp.float32)
        W_out = jax.random.uniform(ks[7], (D_MODEL, D_INNER), minval=-s_xp, maxval=s_xp)
        return {'x': x, 'W_in': W_in, 'conv_w': conv_w, 'conv_b': conv_b, 'W_xproj': W_xproj, 'W_dt': W_dt, 'b_dt': b_dt, 'A_log': A_log, 'D': D, 'W_out': W_out}
    _L0_attn_in = _L0_attn_setup()

    def _L0_ffn_setup():
        import jax, jax.numpy as jnp
        import numpy as np
        D_MODEL = 128
        HIDDEN = 512
        N_EXPERTS = 8
        TOP_K = 2
        key = jax.random.key(seed)
        k_x, k_r, k_w1, k_w2 = jax.random.split(key, 4)
        x = jax.random.normal(k_x, (2, 128, D_MODEL), dtype=jnp.float32)
        Wr = jax.random.normal(k_r, (D_MODEL, N_EXPERTS), dtype=jnp.float32) * 0.02
        W1 = jax.random.normal(k_w1, (N_EXPERTS, D_MODEL, HIDDEN), dtype=jnp.float32) * 0.02
        W2 = jax.random.normal(k_w2, (N_EXPERTS, HIDDEN, D_MODEL), dtype=jnp.float32) * 0.02
        return {'x': x, 'Wr': Wr, 'W1': W1, 'W2': W2}
    _L0_ffn_in = _L0_ffn_setup()
    _d = {'L0_attn_x': _L0_attn_in['x'], 'L0_attn_W_in': _L0_attn_in['W_in'], 'L0_attn_conv_w': _L0_attn_in['conv_w'], 'L0_attn_conv_b': _L0_attn_in['conv_b'], 'L0_attn_W_xproj': _L0_attn_in['W_xproj'], 'L0_attn_W_dt': _L0_attn_in['W_dt'], 'L0_attn_b_dt': _L0_attn_in['b_dt'], 'L0_attn_A_log': _L0_attn_in['A_log'], 'L0_attn_D': _L0_attn_in['D'], 'L0_attn_W_out': _L0_attn_in['W_out'], 'L0_ffn_Wr': _L0_ffn_in['Wr'], 'L0_ffn_W1': _L0_ffn_in['W1'], 'L0_ffn_W2': _L0_ffn_in['W2']}
    _x0 = _d['L0_attn_x']
    _d['L0_attn_x'] = jax.random.normal(jax.random.fold_in(jax.random.key(seed), 1), (8, 512, 128), dtype=_x0.dtype)
    del _x0
    return _d

def reference(L0_attn_x, L0_attn_W_in, L0_attn_conv_w, L0_attn_conv_b, L0_attn_W_xproj, L0_attn_W_dt, L0_attn_b_dt, L0_attn_A_log, L0_attn_D, L0_attn_W_out, L0_ffn_Wr, L0_ffn_W1, L0_ffn_W2):

    def _L0_attn_ref(x, W_in, conv_w, conv_b, W_xproj, W_dt, b_dt, A_log, D, W_out):
        import jax, jax.numpy as jnp
        import numpy as np
        from jax import lax
        D_MODEL, D_STATE, D_CONV, EXPAND = (128, 16, 4, 2)
        D_INNER = EXPAND * D_MODEL
        B, L = (2, 256)
        b, l, _ = x.shape
        d_state = A_log.shape[1]
        d_conv = conv_w.shape[-1]
        xz = x @ W_in.T
        x_in, z = jnp.split(xz, 2, axis=-1)
        lhs = jnp.pad(x_in.transpose(0, 2, 1), ((0, 0), (0, 0), (d_conv - 1, 0)))
        conv = lax.conv_general_dilated(lhs, conv_w, window_strides=(1,), padding='VALID', dimension_numbers=('NCW', 'OIW', 'NCW'), feature_group_count=conv_w.shape[0])
        x_conv = jax.nn.silu(conv.transpose(0, 2, 1) + conv_b)
        ssm_in = x_conv @ W_xproj.T
        dt_raw = ssm_in[..., :1]
        B_ssm = ssm_in[..., 1:1 + d_state]
        C_ssm = ssm_in[..., 1 + d_state:]
        delta = jax.nn.softplus(dt_raw @ W_dt.T + b_dt)
        A = -jnp.exp(A_log)
        deltaA = jnp.exp(delta[..., None] * A)
        deltaB_u = delta[..., None] * B_ssm[:, :, None, :] * x_conv[..., None]

        def step(h, inp):
            dA, dBu, c = inp
            h = dA * h + dBu
            y = jnp.einsum('bds,bs->bd', h, c)
            return (h, y)
        h0 = jnp.zeros((b, deltaA.shape[2], d_state), dtype=x.dtype)
        _, ys = lax.scan(step, h0, (deltaA.transpose(1, 0, 2, 3), deltaB_u.transpose(1, 0, 2, 3), C_ssm.transpose(1, 0, 2)))
        y = ys.transpose(1, 0, 2) + x_conv * D
        y = y * jax.nn.silu(z)
        return y @ W_out.T

    def _L0_ffn_ref(x, Wr, W1, W2):
        import jax, jax.numpy as jnp
        import numpy as np
        D_MODEL = 128
        HIDDEN = 512
        N_EXPERTS = 8
        TOP_K = 2
        B, S, D = x.shape
        flat = x.reshape(-1, D)
        logits = flat @ Wr
        top_vals, top_idx = jax.lax.top_k(logits, TOP_K)
        weights = jax.nn.softmax(top_vals, axis=-1)
        top1 = top_idx[:, 0]
        w_top1 = weights[:, 0]
        h = jax.nn.gelu(jnp.einsum('td,edh->teh', flat, W1), approximate=False)
        y = jnp.einsum('teh,ehd->ted', h, W2)
        y_sel = jnp.take_along_axis(y, top1[:, None, None], axis=1)[:, 0, :]
        out = (w_top1[:, None] * y_sel).reshape(B, S, D)
        return out
    x = L0_attn_x
    x = _layernorm(x + _L0_attn_ref(x, L0_attn_W_in, L0_attn_conv_w, L0_attn_conv_b, L0_attn_W_xproj, L0_attn_W_dt, L0_attn_b_dt, L0_attn_A_log, L0_attn_D, L0_attn_W_out), axis=-1)
    x = _layernorm(x + _L0_ffn_ref(x, L0_ffn_Wr, L0_ffn_W1, L0_ffn_W2), axis=-1)
    return x

_drawn_inputs = setup_inputs


def setup_inputs(seed=0):
    import zlib

    import numpy as np

    out = dict(_drawn_inputs(seed))
    spreads = {'L0_attn_D': (1.0, 0.6)}
    factors = {'L0_attn_W_xproj': 8.0, 'L0_attn_W_dt': 8.0, 'L0_attn_b_dt': 8.0, 'L0_attn_A_log': 8.0}
    for name, (base, spread) in spreads.items():
        noise = np.random.default_rng([zlib.crc32(name.encode()), seed]).standard_normal(out[name].shape)
        drawn = base * np.exp(spread * noise) if base else spread * noise
        out[name] = jnp.asarray(drawn.astype(out[name].dtype))
    for name, factor in factors.items():
        out[name] = (out[name] * factor).astype(out[name].dtype)
    return out
```

```python
import concourse.bass as bass
from concourse import mybir
from contextlib import ExitStack

F32 = mybir.dt.float32
BF16 = mybir.dt.bfloat16
ALU = mybir.AluOpType
ACT = mybir.ActivationFunctionType

P = 128
B, L, DM = 8, 512, 128
DI, NS, KC = 256, 16, 4
NH = DI // P
TT = L // P
NT = B * TT
EPS = 1e-5
NE, HID = 8, 512
HC = HID // P
NSL = -(-(NT + NE - 1) // 4) * 4
RING = 4
GT = 4
NG = NT // GT

LOG_PQ = [(1.0093576036046876, 1.1060657414085027), (-0.08225355201896584, 3.257478545131043),
          (-1.42473938465796, 2.7021118179052617), (-2.321691391327299, 0.43240818485899907)]
LOG_C = 0.005232626352594947


class Batch:

    def __init__(self, pair, base):
        self.pair, self.base = pair, base
        self.n = 2 * pair + base
        self.turn = pair + base // 2
        self.par = base % 2

    def step(self, d):
        return Batch(self.pair, self.base + d)

    def unit(self, s):
        return self.n * NS + s


class Tile:

    def __init__(self, four, base):
        self.base = base
        self.n = RING * four + base
        self.turn = four + base // RING


def wait(eng, sem, value):
    if isinstance(value, int) and value <= 0:
        return
    eng.wait_ge(sem, value)


def build(nc, x, xT, winN, winzT, conv_w, conv_b, wxT, w_dt, b_dt, a_log, d_skip, woutT, wr, w1, w2, out):
    ctx = ExitStack()
    with ctx:
        def sb(name, shape, dt=F32):
            return ctx.enter_context(nc.sbuf_tensor(name, shape, dt))

        def pb(name, shape, dt=F32):
            return ctx.enter_context(nc.psum_tensor(name, shape, dt))

        def sem(name):
            return ctx.enter_context(nc.semaphore(name))

        win_nat = sb("win_nat", [P, NH, DM])
        winz = sb("winz", [P, DI])
        cw = sb("cw", [P, NH, KC])
        cb = sb("cb", [P, NH])
        wx = sb("wx", [P, NH, 1 + 2 * NS])
        wdt = sb("wdt", [P, NH])
        bdt = sb("bdt", [P, NH])
        alog = sb("alog", [P, NH, NS])
        A = sb("A", [P, NH, NS])
        dsk = sb("dsk", [P, NH])
        wout = sb("wout", [P, NH, DM])
        ident = sb("ident", [P, P])
        diagw = sb("diagw", [P, NH, KC, P])
        wconv = sb("wconv", [P, NH, KC, P])
        wbc = sb("wbc", [P, NH, 3, 2 * NS])
        wdtb = sb("wdtb", [P, NH, P])
        pick = sb("pick", [96, 2 * NS, P], BF16)
        rows = sb("rows", [P, 2 * NS])
        logp = sb("logp", [P, len(LOG_PQ)])
        half_neg = sb("half_neg", [P, TT])
        xTb = sb("xTb", [P, 2, KC - 1 + L])
        xtok = sb("xtok", [P, 2, TT, DM])
        cx = sb("cx", [P, NH, L])
        xc = sb("xc", [P, 2, NH, L])
        zraw = sb("zraw", [P, NH, L])
        sz = sb("sz", [P, 2, NH, L])
        relu = sb("relu", [P, NH, L])
        ex = sb("ex", [P, NH, L])
        sq = sb("sq", [P, 4, NH, L])
        delta = sb("delta", [P, 2, NH, L])
        u = sb("u", [P, 2, NH, L])
        parts = sb("parts", [96, 2, L], BF16)
        rest = sb("rest", [96, L])
        mid = sb("mid", [96, L], BF16)
        y2 = sb("y2", [P, NH, L])
        yg = sb("yg", [P, NH, L])
        rs = sb("rs", [P, TT, DM])
        st = sb("st", [P, TT, 6])
        mv = sb("mv", [P, TT, 2])
        vare = sb("vare", [P, TT])
        rstd = sb("rstd", [P, TT])
        NB4 = 4
        da = sb("da", [P, NB4, NH, L])
        hs = sb("hs", [P, NB4, NH, L])
        hc = sb("hc", [P, NB4, NH, L])
        csb = sb("csb", [P, NB4, L])
        x1 = sb("x1", [P, NT, DM])

        w1_sb = hs[:, :, :, :].rearrange("p b h t -> p (b h t)")
        w2_sb = hc[:, :, :, :].rearrange("p b h t -> p (b h t)")
        hid = da[:, 0:2, :, :].rearrange("p b h t -> p (b h) t")
        hidT = da[:, 2:4, :, :].rearrange("p b h t -> p (b h) t")
        yt = sq[:, 0:1, :, :].rearrange("p a h (i c) -> p (a h) i c", c=DM)
        r2 = sq[:, 1:2, :, :].rearrange("p a h (i c) -> p (a h) i c", c=DM)
        xs_sb = sq[:, 2, 0, :].rearrange("p (i c) -> p i c", c=DM)
        xsT = sq[:, 2, 1, :].rearrange("p (i c) -> p i c", c=P)
        ys_sb = sq[:, 3, 0, :].rearrange("p (i c) -> p i c", c=DM)
        wr_sb = sb("wr_sb", [P, NE])
        zero = sb("zero", [P, DM])
        tri = sb("tri", [P, P], BF16)
        ones = sb("ones", [P, P], BF16)
        x1T = sb("x1T", [P, 2, GT * P])
        key8 = sb("key8", [P, NT, NE])
        lgt = sb("lgt", [P, NT, NE])
        m1 = sb("m1", [P, NT])
        m2 = sb("m2", [P, NT])
        kmax = sb("kmax", [P, NT])
        key = sb("key", [P, NT, NE])
        hot = sb("hot", [P, NT, NE])
        hotb = sb("hotb", [P, NE, NT], BF16)
        restl = sb("restl", [P, NT, NE])
        carry = sb("carry", [P, NE, NT])
        upto = sb("upto", [P, NE, NT])
        pos = sb("pos", [P, NE, NT])
        cnti = sb("cnti", [P, NE], mybir.dt.int32)
        tiles = sb("tiles", [P, NE])
        ends = sb("ends", [P, NE])
        start = sb("start", [P, NE])
        slotf = sb("slotf", [P, NT])
        slot = sb("slot", [P, NT], mybir.dt.uint32)
        tno = sb("tno", [1, NSL, NE])
        past = sb("past", [1, NSL, NE])
        expf = sb("expf", [1, NSL])
        exps = sb("exps", [1, NSL], mybir.dt.int32)
        wtop = sb("wtop", [P, NT])
        st2 = sb("st2", [P, 2, GT, 6])
        mv2 = sb("mv2", [P, 2, GT, 2])
        sd2 = sb("sd2", [P, 2, GT])
        rs2 = sb("rs2", [P, 2, GT])
        ones_f = sb("ones_f", [P, NE])
        trif = sb("trif", [P, P])
        iot = sb("iot", [P, NT, NE], mybir.dt.int32)
        tnoi = sb("tnoi", [1, NSL, NE], mybir.dt.int32)
        epsb = sb("epsb", [P, 1])
        xs_d = nc.dram_tensor("sorted_tokens", (NSL * P, DM), F32, kind="Internal").ap()
        ys_d = nc.dram_tensor("sorted_results", (NSL * P, DM), F32, kind="Internal").ap()

        BU = [pb(f"BU{i}", [P, NH, L]) for i in range(2)]
        CB = pb("CB", [P, L])
        Y = pb("Y", [P, NH, L])
        PJ = pb("PJ", [P, L])

        s_w = sem("weights_in")
        s_id = sem("ident_made")
        s_pick = sem("pick_made")
        s_rows = sem("rows_made")
        s_diag = sem("diag_made")
        s_prep = sem("dve_prep")
        s_wcp = sem("wconv_product")
        s_wcc = sem("wconv_copied")
        s_A = sem("A_made")
        s_xT = [sem(f"xT_in{i}") for i in range(2)]
        s_xt = [sem(f"xtok_in{i}") for i in range(2)]
        s_conv = sem("conv_ready")
        s_cx = sem("conv_copied")
        s_xc = sem("xconv_ready")
        s_dt = sem("dt_ready")
        s_dtu = sem("dt_read")
        s_e = sem("exp_small_ready")
        s_sq = sem("squares_ready")
        s_lg = sem("log_steps")
        s_dl = sem("delta_ready")
        s_u = sem("u_ready")
        s_bc = sem("bc_ready")
        s_hi = sem("bc_high")
        s_rest = sem("bc_rest")
        s_mid = sem("bc_mid")
        s_lo = sem("bc_low")
        s_z = sem("z_ready")
        s_zr = sem("z_copied")
        s_sz = sem("silu_z_ready")
        s_B = sem("B_spread")
        s_C = sem("C_spread")
        s_Cc = sem("C_copied")
        s_a = sem("decay_ready")
        s_ub = sem("ub_ready")
        s_h = sem("h_ready")
        s_hc = sem("hc_ready")
        s_y = sem("y_summed")
        s_y2 = sem("y_skip_added")
        s_yg = sem("y_gated")
        s_o = sem("out_ready")
        s_oa = sem("residual_added")
        s_st = sem("stats")
        s_mv = sem("mean_var")
        s_ve = sem("variance_eps_ready")
        s_rstd = sem("rstd_ready")
        s_x1 = sem("x1_ready")
        s_out = [sem(f"stored{i}") for i in range(2)]
        s_we = sem("expert_weights_in")
        s_zs = sem("zero_made")
        s_zf = sem("sorted_tokens_cleared")
        s_carry = sem("carry_ones")
        s_iot = sem("index_patterns")
        s_tri = sem("route_constants")
        s_xTp = sem("x1_transposed")
        s_xTc = sem("x1_transpose_copied")
        s_lo8 = sem("logits_ready")
        s_rt = sem("routing_steps")
        s_hot = sem("hot_ready")
        s_rank = sem("ranks_ready")
        s_slot = sem("slots_ready")
        s_dd = sem("second_minus_first_ready")
        s_ed = sem("exp_difference_ready")
        s_wt = sem("weights_ready")
        s_sc = sem("tokens_sorted")
        s_xs = [sem(f"sorted_tile_in{i}") for i in range(RING)]
        s_tx = sem("sorted_tile_transposed")
        s_txc = sem("sorted_tile_copied")
        s_m1 = sem("hidden_ready")
        s_ge = sem("gelu_ready")
        s_th = sem("hidden_transposed")
        s_thc = sem("hidden_copied")
        s_m2 = sem("result_ready")
        s_yc = sem("result_copied")
        s_ys = [sem(f"result_stored{i}") for i in range(RING)]
        s_g = [sem(f"results_gathered{i}") for i in range(2)]
        s_r2 = sem("residual2_added")
        s_st2 = sem("stats2")
        s_mv2 = sem("mean_var2")
        s_sd = sem("deviation_ready")
        s_rc = sem("reciprocal_ready")
        s_fin = sem("final_ready")

        block = ctx.enter_context(nc.Block())

        def sequences(eng, body, last):
            body(Batch(0, 0))
            with eng.Fori(0, (B - 2) // 2) as pair:
                body(Batch(pair, 1))
                body(Batch(pair, 2))
            last(Batch(0, B - 1))

        def sorted_tiles(eng, step):
            for i in range(RING):
                step(0, i)
            with eng.Fori(1, NSL // RING - 1) as four:
                for i in range(RING):
                    step(four, i)
            for i in range(RING):
                step(NSL // RING - 1, i)

        @block.sync
        def _(sp):
            for dst, src in ((win_nat[:, :, :], winN), (winz[:, :], winzT), (cw[:, :, :], conv_w),
                             (cb[:, :], conv_b), (wx[:, :, :], wxT), (wdt[:, :], w_dt), (bdt[:, :], b_dt),
                             (alog[:, :, :], a_log), (dsk[:, :], d_skip), (wout[:, :, :], woutT)):
                sp.dma_start(dst, src).then_inc(s_w, 16)

            sp.dma_start(wr_sb[:, :], wr).then_inc(s_we, 16)
            sp.wait_ge(s_zs, 1)
            sp.dma_start(xs_d.rearrange("(j p) c -> p j c", p=P),
                         zero[:, :].unsqueeze(1).to_broadcast([P, NSL, DM])).then_inc(s_zf, 16)

            def load(b):
                wait(sp, s_z, 2 * (b.n - 1))
                sp.dma_start(xTb[:, b.par, KC - 1:], xT[:, bass.ds(b.n, 1), :].rearrange("p a t -> p (a t)")).then_inc(s_xT[b.par], 16)
                wait(sp, s_oa, b.n - 1)
                sp.dma_start(xtok[:, b.par, :, :], x[:, bass.ds(b.n * TT, TT), :]).then_inc(s_xt[b.par], 16)

            load(Batch(0, 0))
            load(Batch(0, 1))
            with sp.Fori(0, (B - 2) // 2) as pair:
                load(Batch(pair, 2))
                load(Batch(pair, 3))
            sp.wait_ge(s_hc, B * NS)
            sp.dma_start(w1_sb.rearrange("p (e h) -> p e h", e=NE), w1).then_inc(s_we, 16)
            sp.wait_ge(s_y, B * NS)
            sp.dma_start(w2_sb.rearrange("p (e k c) -> p e k c", e=NE, k=HC), w2).then_inc(s_we, 16)

            def load_tile(j, k):
                wait(sp, s_tx, j - RING + 1)
                sp.dma_start(xs_sb[:, k, :], xs_d[bass.ds(j * P, P), :]).then_inc(s_xs[k], 16)

            def store_tile(j, k):
                sp.wait_ge(s_yc, j + 1)
                sp.dma_start(ys_d[bass.ds(j * P, P), :], ys_sb[:, k, :]).then_inc(s_ys[k], 16)

            sp.wait_ge(s_sc, 16 * NT)
            for j in range(RING):
                load_tile(j, j)
            def step(four, i):
                j = RING * four + i
                if not isinstance(j, int) or j + RING < NSL:
                    load_tile(j + RING, i)
                store_tile(j, i)

            sorted_tiles(sp, step)
            for g in range(NG):
                sp.wait_ge(s_fin, GT * (g + 1))
                if g >= 2:
                    sp.wait_ge(s_out[g % 2], 16 * (g // 2))
                sp.dma_start(out[:, g * GT:(g + 1) * GT, :], r2[:, g % 2, :, :]).then_inc(s_out[g % 2], 16)
            for i in range(2):
                sp.wait_ge(s_out[i], 16 * NG // 2)

        @block.tensor
        def _(pe):
            pe.wait_ge(s_diag, NH * KC)
            pe.wait_ge(s_w, 160)
            for h in range(NH):
                if h:
                    pe.wait_ge(s_wcc, h)
                for k in range(KC):
                    last = nc.tensor.matmul(PJ[:, k * P:(k + 1) * P], win_nat[:, h, :], diagw[:, h, k, :],
                                            start=True, stop=True)
                last.then_inc(s_wcp, 1)
            pe.wait_ge(s_wcc, NH)

            def conv(b, h):
                if h == 0:
                    pe.wait_ge(s_xT[b.par], 16 * (b.turn + 1))
                    wait(pe, s_zr, 2 * b.n)
                else:
                    pe.wait_ge(s_cx, 2 * b.n + 1)
                for k in range(KC):
                    last = nc.tensor.matmul(PJ[:, :], wconv[:, h, k, :], xTb[:, b.par, k:k + L],
                                            start=(k == 0), stop=(k == KC - 1))
                last.then_inc(s_conv, 1)

            def dt(b):
                pe.wait_ge(s_xc, b.n + 1)
                for h in range(NH):
                    last = nc.tensor.matmul(PJ[:, :], wdtb[:, h, :], xc[:, b.par, h, :],
                                            start=(h == 0), stop=(h == NH - 1))
                last.then_inc(s_dt, 1)

            def bc(b):
                pe.wait_ge(s_dtu, 4 * (b.n + 1))
                for h in range(NH):
                    last = nc.tensor.matmul(PJ[0:96, :], wbc[:, h, :, :].rearrange("p a s -> p (a s)"),
                                            xc[:, b.par, h, :], start=(h == 0), stop=(h == NH - 1))
                last.then_inc(s_bc, 1)

            def z(b, h):
                if h == 0:
                    pe.wait_ge(s_rest, b.n + 1)
                    wait(pe, s_oa, b.n - 1)
                else:
                    pe.wait_ge(s_zr, 2 * b.n + 1)
                nc.tensor.matmul(PJ[:, :], winz[:, h * P:(h + 1) * P], xTb[:, b.par, KC - 1:],
                                 start=True, stop=True).then_inc(s_z, 1)

            def out_proj(b, after_rest):
                pe.wait_ge(s_yg, b.n + 1)
                if after_rest:
                    pe.wait_ge(s_rest, b.n + 3)
                for j in range(TT):
                    for h in range(NH):
                        last = nc.tensor.matmul(PJ[:, j * P:(j + 1) * P], yg[:, h, j * P:(j + 1) * P],
                                                wout[:, h, :], start=(h == 0), stop=(h == NH - 1))
                last.then_inc(s_o, 1)

            def spread_b(b, s):
                n = b.unit(s)
                if s == 0:
                    pe.wait_ge(s_lo, b.n + 1)
                wait(pe, s_h, n - 1)
                for h in range(NH):
                    last = nc.tensor.matmul(BU[s % 2][:, h, :], pick[:, s, :], parts[:, b.par, :],
                                            start=True, stop=True)
                last.then_inc(s_B, 1)

            def spread_c(b, s):
                n = b.unit(s)
                if s == 0:
                    pe.wait_ge(s_lo, b.n + 1)
                wait(pe, s_Cc, n)
                nc.tensor.matmul(CB[:, :], pick[:, NS + s, :], parts[:, b.par, :],
                                 start=True, stop=True).then_inc(s_C, 1)

            def y_sum(b, s):
                n = b.unit(s)
                if s == 0:
                    wait(pe, s_y2, 2 * b.n)
                pe.wait_ge(s_hc, n + 1)
                for h in range(NH):
                    last = nc.tensor.matmul(Y[:, h, :], ident[:, :], hc[:, s % NB4, h, :],
                                            start=(s == 0), stop=(s == NS - 1))
                last.then_inc(s_y, 1)

            pe.wait_ge(s_pick, 1)
            pe.wait_ge(s_prep, 3)
            first = Batch(0, 0)
            conv(first, 0)
            conv(first, 1)
            dt(first)
            bc(first)
            z(first, 0)
            z(first, 1)
            spread_c(first, 0)
            spread_c(first, 1)

            def slot(b, s, more):
                spread_b(b, s)
                if s + 2 < NS:
                    spread_c(b, s + 2)
                elif more:
                    spread_c(b.step(1), s + 2 - NS)
                if s >= 3:
                    y_sum(b, s - 3)
                elif not (isinstance(b.n, int) and b.n == 0):
                    y_sum(b.step(-1), s - 3 + NS)

            def body(b):
                nb = b.step(1)
                for s in range(NS):
                    slot(b, s, True)
                    if s == 0:
                        conv(nb, 0)
                    if s == 2:
                        conv(nb, 1)
                    if s == 5:
                        dt(nb)
                    if s == 7:
                        bc(nb)
                    if s == 10 and not (isinstance(b.n, int) and b.n == 0):
                        out_proj(b.step(-1), True)
                    if s == 11:
                        z(nb, 0)
                    if s == 13:
                        z(nb, 1)

            def last_body(b):
                for s in range(NS):
                    slot(b, s, False)
                    if s == 6:
                        pe.wait_ge(s_zr, 2 * B)
                        out_proj(b.step(-1), False)
                for s in range(NS - 3, NS):
                    y_sum(b, s)
                pe.wait_ge(s_oa, B - 1)
                out_proj(b, False)

            sequences(pe, body, last_body)

            def logits(g):
                pe.wait_ge(s_xTc, g + 1)
                for i in range(GT):
                    t = g * GT + i
                    last = nc.tensor.matmul(CB[:, t * NE:(t + 1) * NE], x1T[:, g % 2, i * P:(i + 1) * P],
                                            wr_sb[:, :], start=True, stop=True)
                last.then_inc(s_lo8, 1)

            pe.wait_ge(s_we, 48)
            pe.wait_ge(s_tri, 7)
            pe.wait_ge(s_Cc, B * NS)
            pe.wait_ge(s_h, B * NS)
            pe.wait_ge(s_y2, 2 * B)
            for g in range(NG):
                pe.wait_ge(s_x1, GT * (g + 1))
                wait(pe, s_xTc, g - 1)
                for i in range(GT):
                    last = nc.tensor.transpose(BU[0][:, g % 2, i * P:(i + 1) * P], x1[:, g * GT + i, :], ident[:, :])
                last.then_inc(s_xTp, 1)
                if g:
                    logits(g - 1)
            logits(NG - 1)
            pe.wait_ge(s_hot, 1)
            hot_all = hotb[:, :, :].rearrange("p e i -> p (e i)")
            nc.tensor.matmul(Y[:, 0, 0:NE * NT], tri[:, :], hot_all, start=True, stop=True).then_inc(s_rank, 1)
            nc.tensor.matmul(Y[:, 1, 0:NE * NT], ones[:, :], hot_all, start=True, stop=True).then_inc(s_rank, 1)

            def tile_in(j, k):
                pe.wait_ge(s_xs[k], 16 * (j.turn + 1))
                wait(pe, s_txc, j.n)
                nc.tensor.transpose(CB[:, 0:P], xs_sb[:, k, :], ident[:, :]).then_inc(s_tx, 1)

            def up(jn, k):
                e = pe.value_load(exps[0:1, bass.ds(jn, 1)], min_val=0, max_val=NE - 1)
                pe.wait_ge(s_txc, jn + 1)
                wait(pe, s_ge, jn - 1)
                nc.tensor.matmul(BU[0][:, k % 2, :], xsT[:, k, :], w1_sb[:, bass.ds(e * HID, HID)],
                                 start=True, stop=True).then_inc(s_m1, 1)

            def turn_hidden(jn, k):
                pe.wait_ge(s_ge, jn + 1)
                wait(pe, s_thc, jn - 1)
                for c in range(HC):
                    last = nc.tensor.transpose(BU[1][:, k % 2, c * P:(c + 1) * P], hid[:, k, c * P:(c + 1) * P],
                                               ident[:, :])
                last.then_inc(s_th, 1)

            def down(jn, k):
                e = pe.value_load(exps[0:1, bass.ds(jn, 1)], min_val=0, max_val=NE - 1)
                pe.wait_ge(s_thc, jn + 1)
                wait(pe, s_yc, jn - 1)
                for c in range(HC):
                    last = nc.tensor.matmul(Y[:, k % 2, 0:DM], hidT[:, k, c * P:(c + 1) * P],
                                            w2_sb[:, bass.ds(e * (HC * DM) + c * DM, DM)],
                                            start=(c == 0), stop=(c == HC - 1))
                last.then_inc(s_m2, 1)

            def step(four, i):
                j = RING * four + i
                const = isinstance(j, int)
                if not const or j + 2 < NSL:
                    tile_in(Tile(four, i + 2), (i + 2) % RING)
                if not const or j + 1 < NSL:
                    up(j + 1, (i + 1) % RING)
                turn_hidden(j, i)
                if not const or j >= 1:
                    down(j - 1, (i - 1) % RING)

            pe.wait_ge(s_slot, 2)
            tile_in(Tile(0, 0), 0)
            tile_in(Tile(0, 1), 1)
            up(0, 0)
            sorted_tiles(pe, step)
            down(NSL - 1, (NSL - 1) % RING)

        @block.scalar
        def _(act):
            act.wait_ge(s_w, 160)
            nc.scalar.activation(A[:, :, :], alog[:, :, :], ACT.Exp).then_inc(s_A, 1)
            act.wait_ge(s_A, 1)
            nc.scalar.mul(A[:, :, :], A[:, :, :], -1.0).then_inc(s_A, 1)
            for h in range(NH):
                act.wait_ge(s_wcp, h + 1)
                nc.scalar.copy(wconv[:, h, :, :].rearrange("p k d -> p (k d)"), PJ[:, :]).then_inc(s_wcc, 1)
            act.wait_ge(s_A, 2)
            act.wait_ge(s_prep, 3)

            def copy_conv(b, h):
                act.wait_ge(s_conv, 2 * b.n + h + 1)
                nc.scalar.activation(cx[:, h, :], PJ[:, :], ACT.Identity, bias=cb[:, h:h + 1]).then_inc(s_cx, 1)

            def silu_x(b):
                act.wait_ge(s_cx, 2 * b.n + 2)
                wait(act, s_y2, 2 * (b.n - 1))
                nc.scalar.activation(xc[:, b.par, :, :], cx[:, :, :], ACT.Silu).then_inc(s_xc, 1)

            def silu_z(b):
                act.wait_ge(s_zr, 2 * b.n + 2)
                wait(act, s_yg, b.n - 1)
                nc.scalar.activation(sz[:, b.par, :, :], zraw[:, :, :], ACT.Silu).then_inc(s_sz, 1)

            def softplus_in(b):
                act.wait_ge(s_dt, b.n + 1)
                wait(act, s_dl, b.n)
                for h in range(NH):
                    nc.scalar.activation(ex[:, h, :], PJ[:, :], ACT.Abs, scale=wdt[:, h:h + 1],
                                         bias=bdt[:, h:h + 1]).then_inc(s_dtu, 1)
                    nc.scalar.activation(relu[:, h, :], PJ[:, :], ACT.Relu, scale=wdt[:, h:h + 1],
                                         bias=bdt[:, h:h + 1]).then_inc(s_dtu, 1)

            def softplus_exp(b):
                act.wait_ge(s_dtu, 4 * (b.n + 1))
                nc.scalar.activation(ex[:, :, :], ex[:, :, :], ACT.Exp, scale=-1.0).then_inc(s_e, 1)

            def square(b, i):
                act.wait_ge(s_e, b.n + 1)
                nc.scalar.activation(sq[:, i, :, :], ex[:, :, :], ACT.Square, bias=logp[:, i:i + 1]).then_inc(s_sq, 1)

            def bc_high(b):
                act.wait_ge(s_bc, b.n + 1)
                wait(act, s_B, (b.n - 1) * NS)
                wait(act, s_C, (b.n - 1) * NS)
                nc.scalar.copy(parts[:, b.par, :], PJ[0:96, :]).then_inc(s_hi, 1)

            def bc_mid(b):
                act.wait_ge(s_rest, b.n + 1)
                nc.scalar.copy(parts[32:64, b.par, :], rest[32:64, :]).then_inc(s_mid, 1)
                wait(act, s_lo, b.n)
                nc.scalar.copy(mid[64:96, :], rest[64:96, :]).then_inc(s_mid, 1)

            def copy_z(b, h):
                act.wait_ge(s_z, 2 * b.n + h + 1)
                wait(act, s_sz, b.n)
                nc.scalar.copy(zraw[:, h, :], PJ[:, :]).then_inc(s_zr, 1)

            def decay(b, s):
                n = b.unit(s)
                if s == 0:
                    act.wait_ge(s_dl, b.n + 1)
                wait(act, s_h, n - NB4 + 1)
                for h in range(NH):
                    nc.scalar.activation(da[:, s % NB4, h, 1:], delta[:, b.par, h, 1:], ACT.Exp,
                                         scale=A[:, h, s:s + 1]).then_inc(s_a, 1)

            def copy_c(b, s):
                n = b.unit(s)
                act.wait_ge(s_C, n + 1)
                wait(act, s_hc, n - NB4 + 1)
                nc.scalar.copy(csb[:, s % NB4, :], CB[:, :]).then_inc(s_Cc, 1)

            first = Batch(0, 0)
            copy_conv(first, 0)
            copy_conv(first, 1)
            silu_x(first)
            softplus_in(first)
            softplus_exp(first)
            for i in range(4):
                square(first, i)
            bc_high(first)
            bc_mid(first)
            copy_z(first, 0)
            copy_z(first, 1)

            def body(b):
                nb = b.step(1)
                for s in range(NS):
                    decay(b, s)
                    copy_c(b, s)
                    if s == 2:
                        copy_conv(nb, 0)
                    if s == 4:
                        copy_conv(nb, 1)
                        silu_z(b)
                        silu_x(nb)
                    if s == 7:
                        softplus_in(nb)
                    if s == 8:
                        softplus_exp(nb)
                        square(nb, 0)
                        square(nb, 1)
                    if s == 9:
                        square(nb, 2)
                        square(nb, 3)
                        bc_high(nb)
                    if s == 11:
                        bc_mid(nb)
                    if s == 13:
                        copy_z(nb, 0)
                    if s == 15:
                        copy_z(nb, 1)

            def last_body(b):
                for s in range(NS):
                    decay(b, s)
                    copy_c(b, s)
                    if s == 4:
                        silu_z(b)

            sequences(act, body, last_body)

            for g in range(NG):
                act.wait_ge(s_xTp, g + 1)
                wait(act, s_lo8, g - 1)
                nc.scalar.copy(x1T[:, g % 2, :], BU[0][:, g % 2, :]).then_inc(s_xTc, 1)
            act.wait_ge(s_dd, 1)
            nc.scalar.activation(wtop[:, :], m2[:, :], ACT.Exp).then_inc(s_ed, 1)

            def copy_tile(jn, k):
                act.wait_ge(s_tx, jn + 1)
                wait(act, s_m1, jn - RING + 1)
                nc.scalar.copy(xsT[:, k, :], CB[:, 0:P]).then_inc(s_txc, 1)

            def gelu(jn, k):
                act.wait_ge(s_m1, jn + 1)
                wait(act, s_th, jn - RING + 1)
                nc.scalar.activation(hid[:, k, :], BU[0][:, k % 2, :], ACT.Gelu).then_inc(s_ge, 1)

            copy_tile(0, 0)
            copy_tile(1, 1)
            gelu(0, 0)

            def step(four, i):
                j = RING * four + i
                const = isinstance(j, int)
                if not const or j + 2 < NSL:
                    copy_tile(j + 2, (i + 2) % RING)
                if not const or j + 1 < NSL:
                    gelu(j + 1, (i + 1) % RING)

            sorted_tiles(act, step)
            for g in range(NG):
                act.wait_ge(s_mv2, GT * (g + 1))
                wait(act, s_rc, g - 1)
                nc.scalar.activation(sd2[:, g % 2, :], mv2[:, g % 2, :, 1], ACT.Sqrt, bias=epsb[:, 0:1]).then_inc(s_sd, 1)

        @block.vector
        def _(dve):
            dve.wait_ge(s_w, 160)
            dve.wait_ge(s_id, 2)
            for h in range(NH):
                for k in range(KC):
                    nc.vector.tensor_scalar(diagw[:, h, k, :], ident[:, :], cw[:, h, k:k + 1], None,
                                            ALU.mult).then_inc(s_diag, 1)
            nc.vector.memset(epsb[:, :], EPS).then_inc(s_tri, 1)
            nc.vector.memset(ones[:, :], 1.0).then_inc(s_tri, 1)
            dve.wait_ge(s_iot, 4)
            nc.vector.tensor_copy(tri[:, :], trif[:, :]).then_inc(s_tri, 1)
            nc.vector.tensor_copy(key8[:, :, :], iot[:, :, :]).then_inc(s_tri, 1)
            nc.vector.tensor_copy(tno[:, :, :], tnoi[:, :, :]).then_inc(s_tri, 1)
            nc.vector.memset(ones_f[:, :], 1.0).then_inc(s_tri, 1)
            nc.vector.memset(carry[:, :, :], 1.0).then_inc(s_carry, 1)
            dve.wait_ge(s_carry, 1)
            nc.vector.memset(carry[:, :, 0:1], 0.0).then_inc(s_tri, 1)
            for i, (p, _) in enumerate(LOG_PQ):
                nc.vector.memset(logp[:, i:i + 1], p)
            nc.vector.memset(da[:, :, :, 0:1], 0.0)
            nc.vector.memset(xTb[:, :, 0:KC - 1], 0.0).then_inc(s_prep, 1)
            for i in range(3):
                last = nc.vector.tensor_copy(wbc[:, :, i, :], wx[:, :, 1:])
            last.then_inc(s_prep, 1)
            nc.vector.tensor_copy(wdtb[:, :, :], wx[:, :, 0:1].to_broadcast([P, NH, P])).then_inc(s_prep, 1)

            dve.wait_ge(s_rows, 5)
            nc.vector.tensor_copy(pick[:, :, :], rows[0:96, :].unsqueeze(2).to_broadcast([96, 2 * NS, P])).then_inc(s_pick, 1)

            def bc_rest(b):
                dve.wait_ge(s_hi, b.n + 1)
                wait(dve, s_mid, 2 * b.n)
                nc.vector.tensor_tensor(rest[:, :], PJ[0:96, :], parts[:, b.par, :], ALU.subtract).then_inc(s_rest, 1)

            def bc_low(b):
                dve.wait_ge(s_mid, 2 * b.n + 2)
                nc.vector.tensor_tensor(parts[64:96, b.par, :], rest[64:96, :], mid[64:96, :],
                                        ALU.subtract).then_inc(s_lo, 1)

            def log_step(b, i):
                dve.wait_ge(s_sq, 4 * b.n + i + 1)
                if i:
                    dve.wait_ge(s_lg, 4 * b.n + i)
                before = ex[:, :, :] if i == 0 else sq[:, i - 1, :, :]
                nc.vector.scalar_tensor_tensor(sq[:, i, :, :], sq[:, i, :, :], LOG_PQ[i][1], before,
                                               ALU.add, ALU.mult).then_inc(s_lg, 1)

            def make_delta(b):
                dve.wait_ge(s_lg, 4 * b.n + 4)
                wait(dve, s_a, (b.n - 1) * NS * NH)
                nc.vector.scalar_tensor_tensor(delta[:, b.par, :, :], sq[:, 3, :, :], LOG_C, relu[:, :, :],
                                               ALU.mult, ALU.add).then_inc(s_dl, 1)

            def make_u(b):
                dve.wait_ge(s_dl, b.n + 1)
                nc.vector.tensor_tensor(u[:, b.par, :, :], delta[:, b.par, :, :], xc[:, b.par, :, :],
                                        ALU.mult).then_inc(s_u, 1)

            def make_ub(b, s):
                n = b.unit(s)
                if s == 0:
                    dve.wait_ge(s_u, b.n + 1)
                dve.wait_ge(s_B, n + 1)
                nc.vector.tensor_tensor(BU[s % 2][:, :, :], BU[s % 2][:, :, :], u[:, b.par, :, :],
                                        ALU.mult).then_inc(s_ub, 1)

            def scan(b, s):
                n = b.unit(s)
                dve.wait_ge(s_ub, n + 1)
                dve.wait_ge(s_a, NH * (n + 1))
                wait(dve, s_hc, n - NB4 + 1)
                nc.vector.tensor_tensor_scan(hs[:, s % NB4, :, :].rearrange("p h t -> p (h t)"),
                                             da[:, s % NB4, :, :].rearrange("p h t -> p (h t)"),
                                             BU[s % 2][:, :, :].rearrange("p h t -> p (h t)"),
                                             0.0, ALU.mult, ALU.add).then_inc(s_h, 1)

            def add_skip(b):
                dve.wait_ge(s_y, (b.n + 1) * NS)
                wait(dve, s_yg, b.n)
                for h in range(NH):
                    nc.vector.scalar_tensor_tensor(y2[:, h, :], xc[:, b.par, h, :], dsk[:, h:h + 1], Y[:, h, :],
                                                   ALU.mult, ALU.add).then_inc(s_y2, 1)

            def add_residual(b):
                dve.wait_ge(s_o, b.n + 1)
                dve.wait_ge(s_xt[b.par], 16 * (b.turn + 1))
                wait(dve, s_x1, TT * b.n)
                nc.vector.tensor_tensor(rs[:, :, :].rearrange("p j c -> p (j c)"), PJ[:, :],
                                        xtok[:, b.par, :, :].rearrange("p j c -> p (j c)"),
                                        ALU.add).then_inc(s_oa, 1)

            def stats(b):
                dve.wait_ge(s_oa, b.n + 1)
                for j in range(TT):
                    nc.vector.bn_stats(st[:, j, :], rs[:, j, :]).then_inc(s_st, 1)

            def mean_var(b):
                wait(dve, s_rstd, b.n)
                dve.wait_ge(s_st, TT * (b.n + 1))
                nc.vector.memset(vare[:, :], EPS).then_inc(s_ve, 1)
                for j in range(TT):
                    nc.vector.bn_aggr(mv[:, j, :], st[:, j, :]).then_inc(s_mv, 1)
                dve.wait_ge(s_mv, TT * (b.n + 1))
                dve.wait_ge(s_ve, 2 * b.n + 1)
                nc.vector.tensor_tensor(vare[:, :], mv[:, :, 1], vare[:, :], ALU.add).then_inc(s_ve, 1)

            def normalize(b):
                dve.wait_ge(s_rstd, b.n + 1)
                for j in range(TT):
                    nc.vector.tensor_scalar(x1[:, bass.ds(b.n * TT + j, 1), :].rearrange("p a c -> p (a c)"),
                                            rs[:, j, :], mv[:, j, 0:1], rstd[:, j:j + 1],
                                            ALU.subtract, ALU.mult).then_inc(s_x1, 1)

            first = Batch(0, 0)
            for i in range(4):
                log_step(first, i)
            make_delta(first)
            bc_rest(first)
            bc_low(first)
            make_u(first)
            make_ub(first, 0)

            def body(b):
                nb = b.step(1)
                post = not (isinstance(b.n, int) and b.n == 0)
                for s in range(NS):
                    if s + 1 < NS:
                        make_ub(b, s + 1)
                    else:
                        make_ub(nb, 0)
                    scan(b, s)
                    if s == 2 and post:
                        add_skip(b.step(-1))
                    if 9 <= s < 13:
                        log_step(nb, s - 9)
                    if s == 9:
                        bc_rest(nb)
                    if s == 12:
                        bc_low(nb)
                    if s == 13:
                        make_delta(nb)
                    if s == 14:
                        make_u(nb)
                    if s == 10 and post:
                        add_residual(b.step(-1))
                    if s == 12 and post:
                        stats(b.step(-1))
                    if s == 13 and post:
                        mean_var(b.step(-1))
                    if s == 15 and post:
                        normalize(b.step(-1))

            def last_body(b):
                for s in range(NS):
                    if s + 1 < NS:
                        make_ub(b, s + 1)
                    scan(b, s)
                    if s == 2:
                        add_skip(b.step(-1))
                    if s == 8:
                        add_residual(b.step(-1))
                    if s == 9:
                        stats(b.step(-1))
                    if s == 10:
                        mean_var(b.step(-1))
                    if s == 12:
                        normalize(b.step(-1))
                add_skip(b)
                add_residual(b)
                stats(b)
                mean_var(b)
                normalize(b)

            sequences(dve, body, last_body)

            steps = [0]

            def link(ins):
                steps[0] += 1
                ins.then_inc(s_rt, 1)
                dve.wait_ge(s_rt, steps[0])

            def per_tile(a):
                return a.unsqueeze(2).to_broadcast([P, NT, NE])

            AX = mybir.AxisListType.X
            dve.wait_ge(s_lo8, NG)
            dve.wait_ge(s_tri, 7)
            link(nc.vector.tensor_copy(lgt[:, :, :].rearrange("p t e -> p (t e)"), CB[:, 0:NT * NE]))
            link(nc.vector.tensor_reduce(m1[:, :], lgt[:, :, :], axis=AX, op=ALU.max))
            link(nc.vector.tensor_tensor(key[:, :, :], lgt[:, :, :], per_tile(m1[:, :]), ALU.is_equal))
            link(nc.vector.tensor_tensor(key[:, :, :], key[:, :, :], key8[:, :, :], ALU.mult))
            link(nc.vector.tensor_reduce(kmax[:, :], key[:, :, :], axis=AX, op=ALU.max))
            link(nc.vector.tensor_tensor(hot[:, :, :], key[:, :, :], per_tile(kmax[:, :]), ALU.is_equal))
            nc.vector.tensor_copy(hotb[:, :, :].rearrange("p e t -> p t e"), hot[:, :, :]).then_inc(s_hot, 1)
            link(nc.vector.scalar_tensor_tensor(restl[:, :, :], hot[:, :, :], -3.0e38, lgt[:, :, :], ALU.mult, ALU.add))
            link(nc.vector.tensor_reduce(m2[:, :], restl[:, :, :], axis=AX, op=ALU.max))
            nc.vector.tensor_tensor(m2[:, :], m2[:, :], m1[:, :], ALU.subtract).then_inc(s_dd, 1)
            dve.wait_ge(s_rank, 2)
            link(nc.vector.tensor_tensor_scan(upto[:, :, :].rearrange("p e t -> p (e t)"),
                                              carry[:, :, :].rearrange("p e t -> p (e t)"), Y[:, 1, 0:NE * NT],
                                              0.0, ALU.mult, ALU.add))
            link(nc.vector.tensor_scalar(cnti[:, :], upto[:, :, NT - 1], float(P - 1), None, ALU.add))
            link(nc.vector.tensor_single_scalar(cnti[:, :], cnti[:, :], 7, ALU.logical_shift_right))
            link(nc.vector.tensor_copy(tiles[:, :], cnti[:, :]))
            link(nc.vector.tensor_tensor_scan(ends[:, :], ones_f[:, :], tiles[:, :], 0.0, ALU.mult, ALU.add))
            link(nc.vector.tensor_tensor(start[:, :], ends[:, :], tiles[:, :], ALU.subtract))
            link(nc.vector.tensor_tensor(pos[:, :, :], upto[:, :, :], Y[:, 1, 0:NE * NT].rearrange("p (e t) -> p e t", e=NE),
                                         ALU.subtract))
            link(nc.vector.scalar_tensor_tensor(pos[:, :, :], start[:, :].unsqueeze(2).to_broadcast([P, NE, NT]),
                                                float(P), pos[:, :, :], ALU.mult, ALU.add))
            link(nc.vector.tensor_tensor(pos[:, :, :], pos[:, :, :], Y[:, 0, 0:NE * NT].rearrange("p (e t) -> p e t", e=NE),
                                         ALU.add))
            link(nc.vector.tensor_tensor(pos[:, :, :], pos[:, :, :], hot[:, :, :].rearrange("p t e -> p e t"), ALU.mult))
            link(nc.vector.tensor_reduce(slotf[:, :], pos[:, :, :].rearrange("p e t -> p t e"), axis=AX, op=ALU.add))
            nc.vector.tensor_copy(slot[:, :], slotf[:, :]).then_inc(s_slot, 1)
            link(nc.vector.tensor_tensor(past[:, :, :], tno[:, :, :],
                                         ends[0:1, :].unsqueeze(1).to_broadcast([1, NSL, NE]), ALU.is_ge))
            link(nc.vector.tensor_reduce(expf[:, :], past[:, :, :], axis=AX, op=ALU.add))
            nc.vector.tensor_scalar(exps[:, :], expf[:, :], float(NE - 1), None, ALU.min).then_inc(s_slot, 1)
            dve.wait_ge(s_ed, 1)
            link(nc.vector.tensor_scalar(wtop[:, :], wtop[:, :], 1.0, None, ALU.add))
            link(nc.vector.reciprocal(wtop[:, :], wtop[:, :]))

            def copy_hidden(jn, k):
                dve.wait_ge(s_th, jn + 1)
                wait(dve, s_m2, jn - RING + 1)
                nc.vector.tensor_copy(hidT[:, k, :], BU[1][:, k % 2, :]).then_inc(s_thc, 1)

            def copy_result(j):
                dve.wait_ge(s_m2, j.n + 1)
                wait(dve, s_ys[j.base % RING], 16 * j.turn)
                nc.vector.tensor_copy(ys_sb[:, j.base % RING, :], Y[:, j.base % 2, 0:DM]).then_inc(s_yc, 1)

            copy_hidden(0, 0)

            def step(four, i):
                j = RING * four + i
                if not isinstance(j, int) or j + 1 < NSL:
                    copy_hidden(j + 1, (i + 1) % RING)
                copy_result(Tile(four, i))

            sorted_tiles(dve, step)

            def add_expert(g):
                dve.wait_ge(s_g[g % 2], 16 * GT * (g // 2 + 1))
                if g >= 2:
                    dve.wait_ge(s_out[g % 2], 16 * (g // 2))
                for i in range(GT):
                    t = g * GT + i
                    nc.vector.scalar_tensor_tensor(r2[:, g % 2, i, :], yt[:, g % 2, i, :], wtop[:, t:t + 1],
                                                   x1[:, t, :], ALU.mult, ALU.add).then_inc(s_r2, 1)
                dve.wait_ge(s_r2, GT * (g + 1))
                for i in range(GT):
                    nc.vector.bn_stats(st2[:, g % 2, i, :], r2[:, g % 2, i, :]).then_inc(s_st2, 1)
                dve.wait_ge(s_st2, GT * (g + 1))
                for i in range(GT):
                    nc.vector.bn_aggr(mv2[:, g % 2, i, :], st2[:, g % 2, i, :]).then_inc(s_mv2, 1)

            def final_norm(g):
                dve.wait_ge(s_sd, g + 1)
                nc.vector.reciprocal(rs2[:, g % 2, :], sd2[:, g % 2, :]).then_inc(s_rc, 1)
                dve.wait_ge(s_rc, g + 1)
                for i in range(GT):
                    nc.vector.tensor_scalar(r2[:, g % 2, i, :], r2[:, g % 2, i, :], mv2[:, g % 2, i, 0:1],
                                            rs2[:, g % 2, i:i + 1], ALU.subtract, ALU.mult).then_inc(s_fin, 1)

            for g in range(NG):
                add_expert(g)
                if g:
                    final_norm(g - 1)
            final_norm(NG - 1)

        @block.gpsimd
        def _(pool):
            nc.gpsimd.memset(ident[:, :], 0.0).then_inc(s_id, 1)
            pool.wait_ge(s_id, 1)
            nc.gpsimd.affine_select(out=ident[:, :], in_=ident[:, :], compare_op=ALU.not_equal, fill=1.0, base=0,
                                    pattern=[[-1, P]], channel_multiplier=1).then_inc(s_id, 1)
            nc.gpsimd.memset(half_neg[:, :], -0.5).then_inc(s_rows, 1)
            nc.gpsimd.memset(rows[:, :], 0.0).then_inc(s_rows, 1)
            for i in range(3):
                pool.wait_ge(s_rows, i + 2)
                nc.gpsimd.affine_select(out=rows[:, :], in_=rows[:, :], compare_op=ALU.not_equal, fill=1.0,
                                        base=-2 * NS * i, pattern=[[-1, 2 * NS]],
                                        channel_multiplier=1).then_inc(s_rows, 1)

            nc.gpsimd.memset(zero[:, :], 0.0).then_inc(s_zs, 1)
            nc.gpsimd.iota(iot[:, :, :], pattern=[[0, NT], [-1, NE]], base=NE, channel_multiplier=0).then_inc(s_iot, 1)
            nc.gpsimd.memset(trif[:, :], 1.0).then_inc(s_iot, 1)
            pool.wait_ge(s_iot, 2)
            nc.gpsimd.affine_select(out=trif[:, :], in_=trif[:, :], compare_op=ALU.is_gt, fill=0.0, base=0,
                                    pattern=[[1, P]], channel_multiplier=-1).then_inc(s_iot, 1)
            pool.wait_ge(s_iot, 3)
            nc.gpsimd.iota(tnoi[:, :, :], pattern=[[1, NSL], [0, NE]], base=0, channel_multiplier=0).then_inc(s_iot, 1)
            pool.wait_ge(s_iot, 4)

            def times_c(b, s):
                n = b.unit(s)
                pool.wait_ge(s_h, n + 1)
                pool.wait_ge(s_Cc, n + 1)
                wait(pool, s_y, n - NB4 + 1)
                nc.gpsimd.tensor_tensor(hc[:, s % NB4, :, :], hs[:, s % NB4, :, :],
                                        csb[:, s % NB4, :].unsqueeze(1).to_broadcast([P, NH, L]),
                                        ALU.mult).then_inc(s_hc, 1)

            def gate(b):
                pool.wait_ge(s_y2, 2 * (b.n + 1))
                pool.wait_ge(s_sz, b.n + 1)
                wait(pool, s_o, b.n)
                nc.gpsimd.tensor_tensor(yg[:, :, :], y2[:, :, :], sz[:, b.par, :, :], ALU.mult).then_inc(s_yg, 1)

            def norm(b):
                wait(pool, s_x1, TT * b.n)
                pool.wait_ge(s_ve, 2 * b.n + 2)
                nc.gpsimd.tensor_tensor(rstd[:, :], vare[:, :], half_neg[:, :], ALU.pow).then_inc(s_rstd, 1)

            def body(b):
                post = not (isinstance(b.n, int) and b.n == 0)
                for s in range(NS):
                    times_c(b, s)
                    if s == 3 and post:
                        gate(b.step(-1))
                    if s == 13 and post:
                        norm(b.step(-1))

            def last_body(b):
                for s in range(NS):
                    times_c(b, s)
                    if s == 3:
                        gate(b.step(-1))
                    if s == 11:
                        norm(b.step(-1))
                gate(b)
                norm(b)

            sequences(pool, body, last_body)

            pool.wait_ge(s_slot, 1)
            pool.wait_ge(s_zf, 16)
            pool.wait_ge(s_x1, NT)
            for t in range(NT):
                nc.gpsimd.indirect_dma_start(xs_d, bass.IndirectOffsetOnAxis(ap=slot[:, t:t + 1], axis=0),
                                             x1[:, t, :], None).then_inc(s_sc, 16)
            for k in range(RING):
                pool.wait_ge(s_ys[k], 16 * (NSL // RING))
            for g in range(NG):
                wait(pool, s_r2, GT * (g - 1))
                for i in range(GT):
                    t = g * GT + i
                    nc.gpsimd.indirect_dma_start(yt[:, g % 2, i, :], None, ys_d,
                                                 bass.IndirectOffsetOnAxis(ap=slot[:, t:t + 1], axis=0)
                                                 ).then_inc(s_g[g % 2], 16)


def kernel(**inputs):
    import numpy as np
    import concourse.bacc as bacc
    from concourse.bass_utils import run_bass_kernel_spmd

    nc = bacc.Bacc("TRN2", target_bir_lowering=False, num_devices=1)
    w = {k[3:]: np.asarray(v) for k, v in inputs.items()}
    halves = lambda a: np.ascontiguousarray(a.reshape(NH, P, -1).transpose(1, 0, 2))
    x = w["attn_x"].reshape(B * TT, P, DM)
    arrays = {
        "x": np.ascontiguousarray(x.transpose(1, 0, 2)),
        "xT": np.ascontiguousarray(w["attn_x"].transpose(2, 0, 1)),
        "winN": halves(w["attn_W_in"][:DI]),
        "winzT": np.ascontiguousarray(w["attn_W_in"][DI:].T),
        "conv_w": halves(w["attn_conv_w"]),
        "conv_b": np.ascontiguousarray(halves(w["attn_conv_b"])[:, :, 0]),
        "wxT": halves(np.ascontiguousarray(w["attn_W_xproj"].T)),
        "w_dt": np.ascontiguousarray(halves(w["attn_W_dt"])[:, :, 0]),
        "b_dt": np.ascontiguousarray(halves(w["attn_b_dt"])[:, :, 0]),
        "a_log": halves(w["attn_A_log"]),
        "d_skip": np.ascontiguousarray(halves(w["attn_D"])[:, :, 0]),
        "woutT": halves(np.ascontiguousarray(w["attn_W_out"].T)),
        "wr": np.ascontiguousarray(w["ffn_Wr"]),
        "w1": np.ascontiguousarray(w["ffn_W1"].transpose(1, 0, 2)),
        "w2": np.ascontiguousarray(w["ffn_W2"].reshape(NE, HC, P, DM).transpose(2, 0, 1, 3)),
    }
    args = [nc.dram_tensor(f"in_{k}", v.shape, mybir.dt.from_np(v.dtype), kind="ExternalInput").ap()
            for k, v in arrays.items()]
    out = nc.dram_tensor("out_dram", (P, NT, DM), F32, kind="ExternalOutput").ap()
    build(nc, *args, out)
    r = run_bass_kernel_spmd(nc, [{f"in_{k}": v for k, v in arrays.items()}], core_ids=[0])
    return np.ascontiguousarray(r.results[0]["out_dram"].transpose(1, 0, 2)).reshape(B, L, DM)
```

```python
import concourse.bass as bass
from concourse import mybir
from contextlib import ExitStack

F32 = mybir.dt.float32
BF16 = mybir.dt.bfloat16
ALU = mybir.AluOpType
ACT = mybir.ActivationFunctionType

P = 128
B, L, DM = 8, 512, 128
DI, NS, KC = 256, 16, 4
NH = DI // P
TT = L // P
NT = B * TT
EPS = 1e-5
NE, HID = 8, 512
HC = HID // P
RING = 8
NSL = -(-(NT + NE - 1) // RING) * RING
STAGE = 4
XW = DM + 2
NTOK = NT * P
GT = 4
NG = NT // GT

LOG_PQ = [(1.0093576036046876, 1.1060657414085027), (-0.08225355201896584, 3.257478545131043),
          (-1.42473938465796, 2.7021118179052617), (-2.321691391327299, 0.43240818485899907)]
LOG_C = 0.005232626352594947


class Batch:

    def __init__(self, pair, base):
        self.pair, self.base = pair, base
        self.n = 2 * pair + base
        self.turn = pair + base // 2
        self.par = base % 2
        self.first = isinstance(pair, int) and self.n == 0

    def step(self, d):
        return Batch(self.pair, self.base + d)

    def unit(self, s):
        return self.n * NS + s


class Tile:

    def __init__(self, ring, base):
        self.n = RING * ring + base
        self.const = isinstance(self.n, int)
        self.k, self.turn = base % RING, ring + base // RING
        self.s = base % STAGE
        self.sturn = RING // STAGE * ring + base // STAGE


def wait(eng, sem, value):
    if isinstance(value, int) and value <= 0:
        return
    eng.wait_ge(sem, value)


def build(nc, x, xT, winN, winzT, conv_w, conv_b, wxT, w_dt, b_dt, a_log, d_skip, woutT, wr, w1, w2, out):
    ctx = ExitStack()
    with ctx:
        def sb(name, shape, dt=F32):
            return ctx.enter_context(nc.sbuf_tensor(name, shape, dt))

        def pb(name, shape, dt=F32):
            return ctx.enter_context(nc.psum_tensor(name, shape, dt))

        def sem(name):
            return ctx.enter_context(nc.semaphore(name))

        win_nat = sb("win_nat", [P, NH, DM])
        winz = sb("winz", [P, DI])
        cw = sb("cw", [P, NH, KC])
        cb = sb("cb", [P, NH])
        wx = sb("wx", [P, NH, 1 + 2 * NS])
        wdt = sb("wdt", [P, NH])
        bdt = sb("bdt", [P, NH])
        alog = sb("alog", [P, NH, NS])
        A = sb("A", [P, NH, NS])
        dsk = sb("dsk", [P, NH])
        wout = sb("wout", [P, NH, DM])
        ident = sb("ident", [P, P])
        diagw = sb("diagw", [P, NH, KC, P])
        wconv = sb("wconv", [P, NH, KC, P])
        wbc = sb("wbc", [P, NH, 3, 2 * NS])
        wdtb = sb("wdtb", [P, NH, P])
        pick = sb("pick", [96, 2 * NS, P], BF16)
        rows = sb("rows", [P, 2 * NS])
        logp = sb("logp", [P, len(LOG_PQ)])
        half_neg = sb("half_neg", [P, TT])
        xtok = sb("xtok", [P, 2, TT, DM])
        cx = sb("cx", [P, NH, L])
        xc = sb("xc", [P, 2, NH, L])
        zraw = sb("zraw", [P, NH, L])
        sz = sb("sz", [P, 2, NH, L])
        relu = sb("relu", [P, NH, L])
        ex = sb("ex", [P, NH, L])
        sq = sb("sq", [P, 4, NH, L])
        delta = sb("delta", [P, 2, NH, L])
        u = sb("u", [P, 2, NH, L])
        parts = sb("parts", [96, 2, L], BF16)
        rest = sb("rest", [96, L])
        mid = sb("mid", [96, L], BF16)
        y2 = sb("y2", [P, NH, L])
        yg = sb("yg", [P, NH, L])
        rs = sb("rs", [P, TT, DM])
        st = sb("st", [P, TT, 6])
        mv = sb("mv", [P, TT, 2])
        vare = sb("vare", [P, TT])
        rstd = sb("rstd", [P, TT])
        NB4 = 4
        da = sb("da", [P, NB4, NH, L])
        hs = sb("hs", [P, NB4, NH, L])
        hc = sb("hc", [P, NB4, NH, L])
        crow = sb("crow", [2 * NS, 2, L])
        csb = sb("csb", [P, NB4, L])
        x1 = sb("x1", [P, NT, XW])

        w1_sb = hs[:, :, :, :].rearrange("p b h t -> p (b h t)")
        w2_sb = hc[:, :, :, :].rearrange("p b h t -> p (b h t)")
        hid = da[:, 0:2, :, :].rearrange("p b h t -> p (b h) t")
        hidT = da[:, 2:4, :, :].rearrange("p b h t -> p (b h) t")
        room = sq[:, :, :, :].rearrange("p a h t -> p (a h t)")
        rows_at, turned_at, res_at = 0, RING * XW, RING * XW + STAGE * P
        xs_sb = room[:, rows_at:turned_at].rearrange("p (i c) -> p i c", c=XW)
        xsT = room[:, turned_at:res_at].rearrange("p (i c) -> p i c", c=P)
        res = room[:, res_at:res_at + STAGE * DM].rearrange("p (i c) -> p i c", c=DM)
        xflat = x1[:, :, :].rearrange("p t c -> p (t c)")
        xTs = x1[:, :, :].rearrange("p (b t) c -> p b (t c)", b=B)
        XS = TT * XW
        wr_sb = sb("wr_sb", [P, NE])
        zero = sb("zero", [P, XW])
        tri = sb("tri", [P, P], BF16)
        ones = sb("ones", [P, P], BF16)
        x1T = sb("x1T", [P, 2, GT * P])
        key8 = sb("key8", [P, NT, NE])
        lgt = sb("lgt", [P, NT, NE])
        m1 = sb("m1", [P, NT])
        m2 = sb("m2", [P, NT])
        kmax = sb("kmax", [P, NT])
        key = sb("key", [P, NT, NE])
        hot = sb("hot", [P, NT, NE])
        hotb = sb("hotb", [P, NE, NT], BF16)
        restl = sb("restl", [P, NT, NE])
        carry = sb("carry", [P, NE, NT])
        upto = sb("upto", [P, NE, NT])
        pos = sb("pos", [P, NE, NT])
        cnti = sb("cnti", [P, NE], mybir.dt.int32)
        tiles = sb("tiles", [P, NE])
        ends = sb("ends", [P, NE])
        start = sb("start", [P, NE])
        slotf = sb("slotf", [P, NT])
        slot = sb("slot", [P, NT], mybir.dt.uint32)
        tno = sb("tno", [1, NSL, NE])
        past = sb("past", [1, NSL, NE])
        expf = sb("expf", [1, NSL])
        exps = sb("exps", [1, NSL], mybir.dt.int32)
        wtop = sb("wtop", [P, NT])
        st2 = sb("st2", [P, STAGE, 6])
        mv2 = sb("mv2", [P, STAGE, 2])
        ve2 = sb("ve2", [P, STAGE])
        rs2 = sb("rs2", [P, STAGE])
        num = sb("num", [P, STAGE], mybir.dt.uint32)
        toki = sb("toki", [P, NT], mybir.dt.int32)
        ones_f = sb("ones_f", [P, NE])
        trif = sb("trif", [P, P])
        iot = sb("iot", [P, NT, NE], mybir.dt.int32)
        tnoi = sb("tnoi", [1, NSL, NE], mybir.dt.int32)
        c_d = nc.dram_tensor("C_rows", (2, NS, L), F32, kind="Internal").ap()
        xs_d = nc.dram_tensor("sorted_tokens", (NSL * P, XW), F32, kind="Internal").ap()

        BU = [pb(f"BU{i}", [P, NH, L]) for i in range(2)]
        CB = pb("CB", [P, L])
        Y = pb("Y", [P, NH, L])
        PJ = pb("PJ", [P, L])

        s_w = sem("weights_in")
        s_id = sem("ident_made")
        s_pick = sem("pick_made")
        s_rows = sem("rows_made")
        s_diag = sem("diag_made")
        s_prep = sem("dve_prep")
        s_wcp = sem("wconv_product")
        s_wcc = sem("wconv_copied")
        s_A = sem("A_made")
        s_xT = [sem(f"xT_in{i}") for i in range(2)]
        s_xt = [sem(f"xtok_in{i}") for i in range(2)]
        s_conv = sem("conv_ready")
        s_cx = sem("conv_copied")
        s_xc = sem("xconv_ready")
        s_dt = sem("dt_ready")
        s_dtu = sem("dt_read")
        s_e = sem("exp_small_ready")
        s_sq = sem("squares_ready")
        s_lg = sem("log_steps")
        s_dl = sem("delta_ready")
        s_u = sem("u_ready")
        s_bc = sem("bc_ready")
        s_hi = sem("bc_high")
        s_rest = sem("bc_rest")
        s_mid = sem("bc_mid")
        s_lo = sem("bc_low")
        s_z = sem("z_ready")
        s_zr = sem("z_copied")
        s_sz = sem("silu_z_ready")
        s_B = sem("B_spread")
        s_cr = sem("C_rows_ready")
        s_cd = sem("C_rows_in_dram")
        s_C = [sem(f"C_spread{i}") for i in range(NB4)]
        s_a = sem("decay_ready")
        s_ub = sem("ub_ready")
        s_h = sem("h_ready")
        s_hc = sem("hc_ready")
        s_y = sem("y_summed")
        s_y2 = sem("y_skip_added")
        s_yg = sem("y_gated")
        s_o = sem("out_ready")
        s_oa = sem("residual_added")
        s_st = sem("stats")
        s_mv = sem("mean_var")
        s_ve = sem("variance_eps_ready")
        s_rstd = sem("rstd_ready")
        s_x1 = sem("x1_ready")
        s_out = [sem(f"stored{i}") for i in range(STAGE)]
        s_we = sem("expert_weights_in")
        s_zc = sem("zero_cleared")
        s_zs = sem("zero_made")
        s_zf = sem("sorted_tokens_cleared")
        s_carry = sem("carry_ones")
        s_tok = sem("numbers_in_rows")
        s_iot = sem("index_patterns")
        s_tri = sem("route_constants")
        s_xTp = sem("x1_transposed")
        s_xTc = sem("x1_transpose_copied")
        s_lo8 = sem("logits_ready")
        s_rt = sem("routing_steps")
        s_hot = sem("hot_ready")
        s_rank = sem("ranks_ready")
        s_slot = sem("slots_ready")
        s_dd = sem("second_minus_first_ready")
        s_ed = sem("exp_difference_ready")
        s_wt = sem("weights_ready")
        s_sc = sem("tokens_sorted")
        s_xs = [sem(f"sorted_tile_in{i}") for i in range(RING)]
        s_tx = sem("sorted_tile_transposed")
        s_txc = sem("sorted_tile_copied")
        s_m1 = sem("hidden_ready")
        s_ge = sem("gelu_ready")
        s_th = sem("hidden_transposed")
        s_thc = sem("hidden_copied")
        s_m2 = sem("result_ready")
        s_r2 = sem("residual2_added")
        s_st2 = sem("stats2")
        s_num = sem("token_numbers")
        s_mv2 = sem("mean_var2")
        s_ve2 = sem("variance2_eps")
        s_pw = sem("rstd2_ready")
        s_fin = sem("final_ready")

        block = ctx.enter_context(nc.Block())

        def sequences(eng, body, last):
            body(Batch(0, 0))
            with eng.Fori(0, (B - 2) // 2) as pair:
                body(Batch(pair, 1))
                body(Batch(pair, 2))
            last(Batch(0, B - 1))

        def sorted_tiles(eng, step):
            for i in range(RING):
                step(lambda d, i=i: Tile(0, i + d))
            with eng.Fori(1, NSL // RING - 1) as ring:
                for i in range(RING):
                    step(lambda d, i=i: Tile(ring, i + d))
            for i in range(RING):
                step(lambda d, i=i: Tile(NSL // RING - 1, i + d))

        @block.sync
        def _(sp):
            sp.dma_start(xTs[:, 0, KC - 1:KC - 1 + L], xT[:, 0, :]).then_inc(s_xT[0], 16)
            for dst, src in ((win_nat[:, :, :], winN), (winz[:, :], winzT), (cw[:, :, :], conv_w),
                             (cb[:, :], conv_b), (wx[:, :, :], wxT), (wdt[:, :], w_dt), (bdt[:, :], b_dt),
                             (alog[:, :, :], a_log), (dsk[:, :], d_skip), (wout[:, :, :], woutT),
                             (wr_sb[:, :], wr)):
                sp.dma_start(dst, src).then_inc(s_w, 16)

            sp.dma_start(xTs[:, 1:, KC - 1:KC - 1 + L], xT[:, 1:, :]).then_inc(s_xT[1], 16)
            sp.wait_ge(s_zs, 1)
            sp.dma_start(xs_d.rearrange("(j p) c -> p j c", p=P),
                         zero[:, :].unsqueeze(1).to_broadcast([P, NSL, XW])).then_inc(s_zf, 16)

            def load_tokens(b):
                sp.dma_start(xtok[:, b.par, :, :], x[:, bass.ds(b.n * TT, TT), :]).then_inc(s_xt[b.par], 16)

            def c_out(b):
                sp.wait_ge(s_cr, b.n + 1)
                sp.dma_start(c_d[b.par], crow[NS:2 * NS, b.par, :]).then_inc(s_cd, 16)

            def spread_c(b, s):
                if s == 0:
                    sp.wait_ge(s_cd, 16 * (b.n + 1))
                if s % 2 == 1:
                    wait(sp, s_hc, b.unit(s) - NB4 + 2)
                sp.dma_start(csb[:, s % NB4, :],
                             c_d[b.par, s:s + 1, :].to_broadcast([P, L])).then_inc(s_C[s % NB4], 16)

            load_tokens(Batch(0, 0))
            c_out(Batch(0, 0))

            def body(b):
                for s in range(NS):
                    if s == 12 and not b.first:
                        sp.wait_ge(s_oa, b.n)
                    spread_c(b, s)
                    if s == 12:
                        load_tokens(b.step(1))
                    if s == 14:
                        c_out(b.step(1))

            def last_body(b):
                for s in range(NS):
                    spread_c(b, s)

            sequences(sp, body, last_body)
            sp.wait_ge(s_hc, B * NS)
            sp.dma_start(w1_sb.rearrange("p (e h) -> p e h", e=NE), w1).then_inc(s_we, 16)
            sp.wait_ge(s_y, B * NS * NH)
            sp.dma_start(w2_sb.rearrange("p (e k c) -> p e k c", e=NE, k=HC), w2).then_inc(s_we, 16)

            def load_tile(j):
                wait(sp, s_r2, j.n - RING + 1)
                wait(sp, s_num, j.n - RING + 1)
                sp.dma_start(xs_sb[:, j.k, :], xs_d[bass.ds(j.n * P, P), :]).then_inc(s_xs[j.k], 16)

            sp.wait_ge(s_sc, 16 * NT)
            for j in range(RING):
                load_tile(Tile(0, j))

            def step(tile):
                j = tile(RING)
                if not j.const or j.n < NSL:
                    load_tile(j)

            sorted_tiles(sp, step)

        @block.tensor
        def _(pe):
            pe.wait_ge(s_diag, NH * KC)
            pe.wait_ge(s_w, 176)
            for h in range(NH):
                if h:
                    pe.wait_ge(s_wcc, h)
                for k in range(KC):
                    last = nc.tensor.matmul(PJ[:, k * P:(k + 1) * P], win_nat[:, h, :], diagw[:, h, k, :],
                                            start=True, stop=True)
                last.then_inc(s_wcp, 1)
            pe.wait_ge(s_wcc, NH)

            def conv(b, h, taps=range(KC)):
                if 0 in taps:
                    if h == 0:
                        if b.first:
                            pe.wait_ge(s_xT[0], 16)
                        elif isinstance(b.n, int):
                            pe.wait_ge(s_xT[1], 16)
                        wait(pe, s_zr, 2 * b.n)
                    else:
                        pe.wait_ge(s_cx, 2 * b.n + 1)
                for k in taps:
                    last = nc.tensor.matmul(PJ[:, :], wconv[:, h, k, :], xflat[:, bass.ds(b.n * XS + k, L)],
                                            start=(k == 0), stop=(k == KC - 1))
                if KC - 1 in taps:
                    last.then_inc(s_conv, 1)

            def dt(b):
                pe.wait_ge(s_xc, b.n + 1)
                for h in range(NH):
                    last = nc.tensor.matmul(PJ[:, :], wdtb[:, h, :], xc[:, b.par, h, :],
                                            start=(h == 0), stop=(h == NH - 1))
                last.then_inc(s_dt, 1)

            def bc(b):
                pe.wait_ge(s_dtu, 4 * (b.n + 1))
                for h in range(NH):
                    last = nc.tensor.matmul(PJ[0:96, :], wbc[:, h, :, :].rearrange("p a s -> p (a s)"),
                                            xc[:, b.par, h, :], start=(h == 0), stop=(h == NH - 1))
                last.then_inc(s_bc, 1)

            def z(b, h):
                if h == 0:
                    pe.wait_ge(s_rest, b.n + 1)
                    pe.wait_ge(s_cr, b.n + 1)
                    wait(pe, s_oa, b.n - 1)
                else:
                    pe.wait_ge(s_zr, 2 * b.n + 1)
                nc.tensor.matmul(PJ[:, :], winz[:, h * P:(h + 1) * P], xflat[:, bass.ds(b.n * XS + KC - 1, L)],
                                 start=True, stop=True).then_inc(s_z, 1)

            def out_proj(b, after_rest, tiles=range(TT)):
                if 0 in tiles:
                    pe.wait_ge(s_yg, b.n + 1)
                if after_rest:
                    pe.wait_ge(s_rest, b.n + 3)
                    pe.wait_ge(s_cr, b.n + 3)
                for j in tiles:
                    for h in range(NH):
                        last = nc.tensor.matmul(PJ[:, j * P:(j + 1) * P], yg[:, h, j * P:(j + 1) * P],
                                                wout[:, h, :], start=(h == 0), stop=(h == NH - 1))
                if TT - 1 in tiles:
                    last.then_inc(s_o, 1)

            def spread_b(b, s, h):
                m = NH * b.unit(s) + h
                if s == 0 and h == 0:
                    pe.wait_ge(s_lo, b.n + 1)
                wait(pe, s_h, m - 3)
                nc.tensor.matmul(BU[s % 2][:, h, :], pick[:, s, :], parts[:, b.par, :],
                                 start=True, stop=True).then_inc(s_B, 1)

            def y_sum(b, s, h):
                n = b.unit(s)
                if s == 0:
                    wait(pe, s_y2, 0 if b.first else 2 * b.n + h - 1)
                pe.wait_ge(s_hc, n + 1)
                nc.tensor.matmul(Y[:, h, :], ident[:, :], hc[:, s % NB4, h, :],
                                 start=(s == 0), stop=(s == NS - 1)).then_inc(s_y, 1)

            pe.wait_ge(s_pick, 1)
            pe.wait_ge(s_prep, 3)
            first = Batch(0, 0)
            conv(first, 0)
            conv(first, 1)
            dt(first)
            bc(first)
            z(first, 0)
            z(first, 1)

            YLAG = 4

            def half_slot(b, s, h, more):
                spread_b(b, s, h)
                if s >= YLAG:
                    y_sum(b, s - YLAG, h)
                elif not b.first:
                    y_sum(b.step(-1), s - YLAG + NS, h)

            def body(b):
                nb = b.step(1)
                for s in range(NS):
                    for h in range(NH):
                        half_slot(b, s, h, True)
                        if s in (0, 1):
                            conv(nb, 0, [2 * s + h])
                        if s in (3, 4):
                            conv(nb, 1, [2 * (s - 3) + h])
                        if s == 6 and h == 1:
                            dt(nb)
                        if s == 8 and h == 1:
                            bc(nb)
                        if s in (11, 12) and not b.first:
                            out_proj(b.step(-1), s == 11 and h == 0, [2 * (s - 11) + h])
                        if s == 13 and h == 1:
                            z(nb, 0)
                        if s == 15 and h == 1:
                            z(nb, 1)

            def last_body(b):
                for s in range(NS):
                    for h in range(NH):
                        half_slot(b, s, h, False)
                        if s in (6, 7):
                            if s == 6 and h == 0:
                                pe.wait_ge(s_zr, 2 * B)
                            out_proj(b.step(-1), False, [2 * (s - 6) + h])
                for s in range(NS - YLAG, NS):
                    for h in range(NH):
                        y_sum(b, s, h)
                pe.wait_ge(s_h, B * NS * NH)
                pe.wait_ge(s_tri, 6)
                for g in range(NG - 1):
                    turn_tokens(g)
                    if g:
                        logits(g - 1)
                logits(NG - 2)
                pe.wait_ge(s_oa, B - 1)
                out_proj(b, False)

            def turn_tokens(g):
                pe.wait_ge(s_x1, GT * (g + 1))
                wait(pe, s_xTc, g - 1)
                for i in range(GT):
                    last = nc.tensor.transpose(BU[0][:, g % 2, i * P:(i + 1) * P], x1[:, g * GT + i, 0:DM], ident[:, :])
                last.then_inc(s_xTp, 1)

            def logits(g):
                pe.wait_ge(s_xTc, g + 1)
                for i in range(GT):
                    t = g * GT + i
                    last = nc.tensor.matmul(CB[:, t * NE:(t + 1) * NE], x1T[:, g % 2, i * P:(i + 1) * P],
                                            wr_sb[:, :], start=True, stop=True)
                last.then_inc(s_lo8, 1)

            sequences(pe, body, last_body)


            turn_tokens(NG - 1)
            logits(NG - 1)
            pe.wait_ge(s_y2, 2 * B)
            pe.wait_ge(s_hot, 1)
            hot_all = hotb[:, :, :].rearrange("p e i -> p (e i)")
            nc.tensor.matmul(Y[:, 0, 0:NE * NT], tri[:, :], hot_all, start=True, stop=True).then_inc(s_rank, 1)
            nc.tensor.matmul(Y[:, 1, 0:NE * NT], ones[:, :], hot_all, start=True, stop=True).then_inc(s_rank, 1)

            def tile_in(j):
                pe.wait_ge(s_xs[j.k], 16 * (j.turn + 1))
                wait(pe, s_txc, j.n)
                nc.tensor.transpose(CB[:, 0:P], xs_sb[:, j.k, 0:DM], ident[:, :]).then_inc(s_tx, 1)

            def expert(j):
                return pe.value_load(exps[0:1, bass.ds(j.n, 1)], min_val=0, max_val=NE - 1)

            def up(j):
                e = expert(j)
                pe.wait_ge(s_txc, j.n + 1)
                wait(pe, s_ge, j.n - 1)
                nc.tensor.matmul(BU[0][:, j.k % 2, :], xsT[:, j.s, :], w1_sb[:, bass.ds(e * HID, HID)],
                                 start=True, stop=True).then_inc(s_m1, 1)

            def turn_hidden(j):
                pe.wait_ge(s_ge, j.n + 1)
                wait(pe, s_thc, j.n - 1)
                for c in range(HC):
                    last = nc.tensor.transpose(BU[1][:, j.k % 2, c * P:(c + 1) * P], hid[:, j.s, c * P:(c + 1) * P],
                                               ident[:, :])
                last.then_inc(s_th, 1)

            def down(j):
                e = expert(j)
                pe.wait_ge(s_thc, j.n + 1)
                wait(pe, s_r2, j.n - 1)
                for c in range(HC):
                    last = nc.tensor.matmul(Y[:, j.k % 2, 0:DM], hidT[:, j.s, c * P:(c + 1) * P],
                                            w2_sb[:, bass.ds(e * (HC * DM) + c * DM, DM)],
                                            start=(c == 0), stop=(c == HC - 1))
                last.then_inc(s_m2, 1)

            def step(tile):
                j = tile(0)
                if not j.const or j.n + 2 < NSL:
                    tile_in(tile(2))
                if not j.const or j.n + 1 < NSL:
                    up(tile(1))
                turn_hidden(j)
                if not j.const or j.n >= 1:
                    down(tile(-1))

            pe.wait_ge(s_slot, 2)
            tile_in(Tile(0, 0))
            tile_in(Tile(0, 1))
            pe.wait_ge(s_we, 32)
            up(Tile(0, 0))
            sorted_tiles(pe, step)
            down(Tile(0, NSL - 1))

        @block.scalar
        def _(act):
            act.wait_ge(s_w, 176)
            nc.scalar.activation(A[:, :, :], alog[:, :, :], ACT.Exp).then_inc(s_A, 1)
            act.wait_ge(s_A, 1)
            nc.scalar.mul(A[:, :, :], A[:, :, :], -1.0).then_inc(s_A, 1)
            for h in range(NH):
                act.wait_ge(s_wcp, h + 1)
                nc.scalar.copy(wconv[:, h, :, :].rearrange("p k d -> p (k d)"), PJ[:, :]).then_inc(s_wcc, 1)
            act.wait_ge(s_A, 2)
            act.wait_ge(s_prep, 3)

            def copy_conv(b, h):
                act.wait_ge(s_conv, 2 * b.n + h + 1)
                nc.scalar.activation(cx[:, h, :], PJ[:, :], ACT.Identity, bias=cb[:, h:h + 1]).then_inc(s_cx, 1)

            def silu_x(b):
                act.wait_ge(s_cx, 2 * b.n + 2)
                wait(act, s_y2, 2 * (b.n - 1))
                nc.scalar.activation(xc[:, b.par, :, :], cx[:, :, :], ACT.Silu).then_inc(s_xc, 1)

            def silu_z(b):
                act.wait_ge(s_zr, 2 * b.n + 2)
                wait(act, s_yg, b.n - 1)
                nc.scalar.activation(sz[:, b.par, :, :], zraw[:, :, :], ACT.Silu).then_inc(s_sz, 1)

            def softplus_in(b):
                act.wait_ge(s_dt, b.n + 1)
                wait(act, s_dl, b.n)
                for h in range(NH):
                    nc.scalar.activation(ex[:, h, :], PJ[:, :], ACT.Abs, scale=wdt[:, h:h + 1],
                                         bias=bdt[:, h:h + 1]).then_inc(s_dtu, 1)
                    nc.scalar.activation(relu[:, h, :], PJ[:, :], ACT.Relu, scale=wdt[:, h:h + 1],
                                         bias=bdt[:, h:h + 1]).then_inc(s_dtu, 1)

            def softplus_exp(b):
                act.wait_ge(s_dtu, 4 * (b.n + 1))
                nc.scalar.activation(ex[:, :, :], ex[:, :, :], ACT.Exp, scale=-1.0).then_inc(s_e, 1)

            def square(b, i):
                act.wait_ge(s_e, b.n + 1)
                nc.scalar.activation(sq[:, i, :, :], ex[:, :, :], ACT.Square, bias=logp[:, i:i + 1]).then_inc(s_sq, 1)

            def bc_high(b):
                act.wait_ge(s_bc, b.n + 1)
                wait(act, s_B, (b.n - 1) * NS * NH)
                nc.scalar.copy(parts[:, b.par, :], PJ[0:96, :]).then_inc(s_hi, 1)

            def bc_mid(b):
                act.wait_ge(s_rest, b.n + 1)
                nc.scalar.copy(parts[32:64, b.par, :], rest[32:64, :]).then_inc(s_mid, 1)
                wait(act, s_lo, b.n)
                nc.scalar.copy(mid[64:96, :], rest[64:96, :]).then_inc(s_mid, 1)

            def copy_z(b, h):
                act.wait_ge(s_z, 2 * b.n + h + 1)
                wait(act, s_sz, b.n)
                nc.scalar.copy(zraw[:, h, :], PJ[:, :]).then_inc(s_zr, 1)

            def decay(b, s):
                n = b.unit(s)
                if s == 0:
                    act.wait_ge(s_dl, b.n + 1)
                for h in range(NH):
                    wait(act, s_h, NH * (n - NB4) + h + 1)
                    nc.scalar.activation(da[:, s % NB4, h, :], delta[:, b.par, h, :], ACT.Exp,
                                         scale=A[:, h, s:s + 1]).then_inc(s_a, 1)

            def c_rows(b):
                act.wait_ge(s_bc, b.n + 1)
                for i in range(NB4):
                    wait(act, s_C[i], 16 * (NS // NB4) * (b.n - 1))
                nc.scalar.copy(crow[:, b.par, :], PJ[0:2 * NS, :]).then_inc(s_cr, 1)

            first = Batch(0, 0)
            copy_conv(first, 0)
            copy_conv(first, 1)
            silu_x(first)
            softplus_in(first)
            softplus_exp(first)
            for i in range(4):
                square(first, i)
            bc_high(first)
            c_rows(first)
            bc_mid(first)
            copy_z(first, 0)
            copy_z(first, 1)

            def body(b):
                nb = b.step(1)
                for s in range(NS):
                    decay(b, s)
                    if s == 1 and not b.first:
                        copy_z(b, 1)
                    if s == 4:
                        copy_conv(nb, 0)
                    if s == 7:
                        copy_conv(nb, 1)
                        silu_z(b)
                        silu_x(nb)
                    if s == 9:
                        softplus_in(nb)
                    if s == 10:
                        softplus_exp(nb)
                        square(nb, 0)
                    if s == 11:
                        square(nb, 1)
                        square(nb, 2)
                        bc_high(nb)
                        c_rows(nb)
                    if s == 12:
                        square(nb, 3)
                    if s == 13:
                        bc_mid(nb)
                    if s == 15:
                        copy_z(nb, 0)

            def last_body(b):
                for s in range(NS):
                    decay(b, s)
                    if s == 1:
                        copy_z(b, 1)
                    if s == 4:
                        silu_z(b)

            sequences(act, body, last_body)

            for g in range(NG):
                act.wait_ge(s_xTp, g + 1)
                wait(act, s_lo8, g - 1)
                nc.scalar.copy(x1T[:, g % 2, :], BU[0][:, g % 2, :]).then_inc(s_xTc, 1)
            act.wait_ge(s_dd, 1)
            nc.scalar.activation(wtop[:, :], m2[:, :], ACT.Exp).then_inc(s_ed, 1)

            def copy_tile(j):
                act.wait_ge(s_tx, j.n + 1)
                wait(act, s_m1, j.n - STAGE + 1)
                nc.scalar.copy(xsT[:, j.s, :], CB[:, 0:P]).then_inc(s_txc, 1)

            def gelu(j):
                act.wait_ge(s_m1, j.n + 1)
                wait(act, s_th, j.n - STAGE + 1)
                nc.scalar.activation(hid[:, j.s, :], BU[0][:, j.k % 2, :], ACT.Gelu).then_inc(s_ge, 1)

            def step(tile):
                j = tile(0)
                if not j.const or j.n + 2 < NSL:
                    copy_tile(tile(2))
                if not j.const or j.n + 1 < NSL:
                    gelu(tile(1))

            copy_tile(Tile(0, 0))
            copy_tile(Tile(0, 1))
            gelu(Tile(0, 0))
            sorted_tiles(act, step)

        @block.vector
        def _(dve):
            dve.wait_ge(s_w, 176)
            dve.wait_ge(s_id, 2)
            for h in range(NH):
                for k in range(KC):
                    nc.vector.tensor_scalar(diagw[:, h, k, :], ident[:, :], cw[:, h, k:k + 1], None,
                                            ALU.mult).then_inc(s_diag, 1)
            dve.wait_ge(s_iot, 5)
            nc.vector.memset(ones[:, :], 1.0).then_inc(s_tri, 1)
            dve.wait_ge(s_iot, 4)
            nc.vector.tensor_copy(tri[:, :], trif[:, :]).then_inc(s_tri, 1)
            nc.vector.tensor_copy(key8[:, :, :], iot[:, :, :]).then_inc(s_tri, 1)
            nc.vector.tensor_copy(tno[:, :, :], tnoi[:, :, :]).then_inc(s_tri, 1)
            nc.vector.memset(ones_f[:, :], 1.0).then_inc(s_tri, 1)
            nc.vector.memset(carry[:, :, :], 1.0).then_inc(s_carry, 1)
            dve.wait_ge(s_carry, 1)
            nc.vector.memset(carry[:, :, 0:1], 0.0).then_inc(s_tri, 1)
            for i, (p, _) in enumerate(LOG_PQ):
                nc.vector.memset(logp[:, i:i + 1], p)
            nc.vector.memset(xTs[:, :, 0:KC - 1], 0.0).then_inc(s_prep, 1)
            for i in range(3):
                last = nc.vector.tensor_copy(wbc[:, :, i, :], wx[:, :, 1:])
            last.then_inc(s_prep, 1)
            nc.vector.tensor_copy(wdtb[:, :, :], wx[:, :, 0:1].to_broadcast([P, NH, P])).then_inc(s_prep, 1)

            dve.wait_ge(s_rows, 5)
            nc.vector.tensor_copy(pick[:, :, :], rows[0:96, :].unsqueeze(2).to_broadcast([96, 2 * NS, P])).then_inc(s_pick, 1)

            def bc_rest(b):
                dve.wait_ge(s_hi, b.n + 1)
                dve.wait_ge(s_cr, b.n + 1)
                wait(dve, s_mid, 2 * b.n)
                nc.vector.tensor_tensor(rest[:, :], PJ[0:96, :], parts[:, b.par, :], ALU.subtract).then_inc(s_rest, 1)

            def bc_low(b):
                dve.wait_ge(s_mid, 2 * b.n + 2)
                nc.vector.tensor_tensor(parts[64:96, b.par, :], rest[64:96, :], mid[64:96, :],
                                        ALU.subtract).then_inc(s_lo, 1)

            def log_step(b, i):
                dve.wait_ge(s_sq, 4 * b.n + i + 1)
                if i:
                    dve.wait_ge(s_lg, 4 * b.n + i)
                before = ex[:, :, :] if i == 0 else sq[:, i - 1, :, :]
                nc.vector.scalar_tensor_tensor(sq[:, i, :, :], sq[:, i, :, :], LOG_PQ[i][1], before,
                                               ALU.add, ALU.mult).then_inc(s_lg, 1)

            def make_delta(b):
                dve.wait_ge(s_lg, 4 * b.n + 4)
                wait(dve, s_a, (b.n - 1) * NS * NH)
                nc.vector.scalar_tensor_tensor(delta[:, b.par, :, :], sq[:, 3, :, :], LOG_C, relu[:, :, :],
                                               ALU.mult, ALU.add).then_inc(s_dl, 1)

            def make_u(b):
                dve.wait_ge(s_dl, b.n + 1)
                nc.vector.tensor_tensor(u[:, b.par, :, :], delta[:, b.par, :, :], xc[:, b.par, :, :],
                                        ALU.mult).then_inc(s_u, 1)

            def make_ub(b, s, h):
                if s == 0 and h == 0:
                    dve.wait_ge(s_u, b.n + 1)
                dve.wait_ge(s_B, NH * b.unit(s) + h + 1)
                nc.vector.tensor_tensor(BU[s % 2][:, h, :], BU[s % 2][:, h, :], u[:, b.par, h, :],
                                        ALU.mult).then_inc(s_ub, 1)

            def scan(b, s, h):
                n = b.unit(s)
                dve.wait_ge(s_ub, NH * n + h + 1)
                dve.wait_ge(s_a, NH * n + h + 1)
                if h == 0:
                    wait(dve, s_hc, n - NB4 + 1)
                nc.vector.tensor_tensor_scan(hs[:, s % NB4, h, :], da[:, s % NB4, h, :], BU[s % 2][:, h, :],
                                             0.0, ALU.mult, ALU.add).then_inc(s_h, 1)

            def unit(b, s, more):
                make_ub(b, s, 1)
                scan(b, s, 0)
                if s + 1 < NS:
                    make_ub(b, s + 1, 0)
                elif more:
                    make_ub(b.step(1), 0, 0)
                scan(b, s, 1)

            def add_skip(b):
                wait(dve, s_yg, b.n)
                for h in range(NH):
                    dve.wait_ge(s_y, ((b.n + 1) * NS - 1) * NH + h + 1)
                    nc.vector.scalar_tensor_tensor(y2[:, h, :], xc[:, b.par, h, :], dsk[:, h:h + 1], Y[:, h, :],
                                                   ALU.mult, ALU.add).then_inc(s_y2, 1)

            def add_residual(b):
                dve.wait_ge(s_o, b.n + 1)
                dve.wait_ge(s_xt[b.par], 16 * (b.turn + 1))
                wait(dve, s_x1, TT * b.n)
                nc.vector.tensor_tensor(rs[:, :, :].rearrange("p j c -> p (j c)"), PJ[:, :],
                                        xtok[:, b.par, :, :].rearrange("p j c -> p (j c)"),
                                        ALU.add).then_inc(s_oa, 1)

            def stats(b):
                dve.wait_ge(s_oa, b.n + 1)
                for j in range(TT):
                    nc.vector.bn_stats(st[:, j, :], rs[:, j, :]).then_inc(s_st, 1)

            def mean_var(b):
                wait(dve, s_rstd, b.n)
                dve.wait_ge(s_st, TT * (b.n + 1))
                nc.vector.memset(vare[:, :], EPS).then_inc(s_ve, 1)
                for j in range(TT):
                    nc.vector.bn_aggr(mv[:, j, :], st[:, j, :]).then_inc(s_mv, 1)
                dve.wait_ge(s_mv, TT * (b.n + 1))
                dve.wait_ge(s_ve, 2 * b.n + 1)
                nc.vector.tensor_tensor(vare[:, :], mv[:, :, 1], vare[:, :], ALU.add).then_inc(s_ve, 1)

            def normalize(b):
                dve.wait_ge(s_rstd, b.n + 1)
                for j in range(TT):
                    nc.vector.tensor_scalar(x1[:, bass.ds(b.n * TT + j, 1), 0:DM].rearrange("p a c -> p (a c)"),
                                            rs[:, j, :], mv[:, j, 0:1], rstd[:, j:j + 1],
                                            ALU.subtract, ALU.mult).then_inc(s_x1, 1)

            first = Batch(0, 0)
            for i in range(4):
                log_step(first, i)
            make_delta(first)
            bc_rest(first)
            bc_low(first)
            make_u(first)
            make_ub(first, 0, 0)

            def body(b):
                nb = b.step(1)
                post = not b.first
                for s in range(NS):
                    unit(b, s, True)
                    if s == 2 and post:
                        add_skip(b.step(-1))
                    if 8 <= s < 12:
                        log_step(nb, s - 8)
                    if s == 9:
                        bc_rest(nb)
                    if s == 11:
                        bc_low(nb)
                    if s == 12:
                        make_delta(nb)
                    if s == 13:
                        make_u(nb)
                    if s == 11 and post:
                        add_residual(b.step(-1))
                    if s == 12 and post:
                        stats(b.step(-1))
                    if s == 13 and post:
                        mean_var(b.step(-1))
                    if s == 15 and post:
                        normalize(b.step(-1))

            def last_body(b):
                for s in range(NS):
                    unit(b, s, False)
                    if s == 2:
                        add_skip(b.step(-1))
                    if s == 8:
                        add_residual(b.step(-1))
                    if s == 9:
                        stats(b.step(-1))
                    if s == 10:
                        mean_var(b.step(-1))
                    if s == 12:
                        normalize(b.step(-1))
                add_skip(b)
                add_residual(b)
                stats(b)
                mean_var(b)
                normalize(b)

            sequences(dve, body, last_body)

            steps = [0]

            def link(ins):
                steps[0] += 1
                ins.then_inc(s_rt, 1)
                dve.wait_ge(s_rt, steps[0])

            def per_tile(a):
                return a.unsqueeze(2).to_broadcast([P, NT, NE])

            AX = mybir.AxisListType.X
            nc.vector.tensor_copy(x1[:, :, DM + 1:DM + 2], toki[:, :].unsqueeze(2)).then_inc(s_tok, 1)
            dve.wait_ge(s_lo8, NG)
            dve.wait_ge(s_tri, 6)
            link(nc.vector.tensor_copy(lgt[:, :, :].rearrange("p t e -> p (t e)"), CB[:, 0:NT * NE]))
            link(nc.vector.tensor_reduce(m1[:, :], lgt[:, :, :], axis=AX, op=ALU.max))
            link(nc.vector.tensor_tensor(key[:, :, :], lgt[:, :, :], per_tile(m1[:, :]), ALU.is_equal))
            link(nc.vector.tensor_tensor(key[:, :, :], key[:, :, :], key8[:, :, :], ALU.mult))
            link(nc.vector.tensor_reduce(kmax[:, :], key[:, :, :], axis=AX, op=ALU.max))
            link(nc.vector.tensor_tensor(hot[:, :, :], key[:, :, :], per_tile(kmax[:, :]), ALU.is_equal))
            nc.vector.tensor_copy(hotb[:, :, :].rearrange("p e t -> p t e"), hot[:, :, :]).then_inc(s_hot, 1)
            link(nc.vector.scalar_tensor_tensor(restl[:, :, :], hot[:, :, :], -3.0e38, lgt[:, :, :], ALU.mult, ALU.add))
            link(nc.vector.tensor_reduce(m2[:, :], restl[:, :, :], axis=AX, op=ALU.max))
            nc.vector.tensor_tensor(m2[:, :], m2[:, :], m1[:, :], ALU.subtract).then_inc(s_dd, 1)
            dve.wait_ge(s_rank, 2)
            link(nc.vector.tensor_tensor_scan(upto[:, :, :].rearrange("p e t -> p (e t)"),
                                              carry[:, :, :].rearrange("p e t -> p (e t)"), Y[:, 1, 0:NE * NT],
                                              0.0, ALU.mult, ALU.add))
            link(nc.vector.tensor_scalar(cnti[:, :], upto[:, :, NT - 1], float(P - 1), None, ALU.add))
            link(nc.vector.tensor_single_scalar(cnti[:, :], cnti[:, :], 7, ALU.logical_shift_right))
            link(nc.vector.tensor_copy(tiles[:, :], cnti[:, :]))
            link(nc.vector.tensor_tensor_scan(ends[:, :], ones_f[:, :], tiles[:, :], 0.0, ALU.mult, ALU.add))
            link(nc.vector.tensor_tensor(start[:, :], ends[:, :], tiles[:, :], ALU.subtract))
            link(nc.vector.tensor_tensor(pos[:, :, :], upto[:, :, :], Y[:, 1, 0:NE * NT].rearrange("p (e t) -> p e t", e=NE),
                                         ALU.subtract))
            link(nc.vector.scalar_tensor_tensor(pos[:, :, :], start[:, :].unsqueeze(2).to_broadcast([P, NE, NT]),
                                                float(P), pos[:, :, :], ALU.mult, ALU.add))
            link(nc.vector.tensor_tensor(pos[:, :, :], pos[:, :, :], Y[:, 0, 0:NE * NT].rearrange("p (e t) -> p e t", e=NE),
                                         ALU.add))
            link(nc.vector.tensor_tensor(pos[:, :, :], pos[:, :, :], hot[:, :, :].rearrange("p t e -> p e t"), ALU.mult))
            link(nc.vector.tensor_reduce(slotf[:, :], pos[:, :, :].rearrange("p e t -> p t e"), axis=AX, op=ALU.add))
            nc.vector.tensor_copy(slot[:, :], slotf[:, :]).then_inc(s_slot, 1)
            link(nc.vector.tensor_tensor(past[:, :, :], tno[:, :, :],
                                         ends[0:1, :].unsqueeze(1).to_broadcast([1, NSL, NE]), ALU.is_ge))
            link(nc.vector.tensor_reduce(expf[:, :], past[:, :, :], axis=AX, op=ALU.add))
            nc.vector.tensor_scalar(exps[:, :], expf[:, :], float(NE - 1), None, ALU.min).then_inc(s_slot, 1)
            dve.wait_ge(s_ed, 1)
            link(nc.vector.tensor_scalar(wtop[:, :], wtop[:, :], 1.0, None, ALU.add))
            nc.vector.reciprocal(x1[:, :, DM:DM + 1], wtop[:, :].unsqueeze(2)).then_inc(s_wt, 1)

            def copy_hidden(j):
                dve.wait_ge(s_th, j.n + 1)
                wait(dve, s_m2, j.n - STAGE + 1)
                nc.vector.tensor_copy(hidT[:, j.s, :], BU[1][:, j.k % 2, :]).then_inc(s_thc, 1)

            def add_expert(j):
                dve.wait_ge(s_m2, j.n + 1)
                wait(dve, s_out[j.s], 16 * j.sturn)
                nc.vector.scalar_tensor_tensor(res[:, j.s, :], Y[:, j.k % 2, 0:DM], xs_sb[:, j.k, DM:DM + 1],
                                               xs_sb[:, j.k, 0:DM], ALU.mult, ALU.add).then_inc(s_r2, 1)

            def stats2(j):
                dve.wait_ge(s_r2, j.n + 1)
                nc.vector.bn_stats(st2[:, j.s, :], res[:, j.s, :]).then_inc(s_st2, 1)
                dve.wait_ge(s_st2, j.n + 1)
                nc.vector.tensor_copy(num[:, j.s:j.s + 1], xs_sb[:, j.k, DM + 1:DM + 2]).then_inc(s_num, 1)
                nc.vector.bn_aggr(mv2[:, j.s, :], st2[:, j.s, :]).then_inc(s_mv2, 1)

            def variance2(j):
                dve.wait_ge(s_mv2, j.n + 1)
                wait(dve, s_pw, j.n - STAGE + 1)
                nc.vector.tensor_scalar(ve2[:, j.s:j.s + 1], mv2[:, j.s, 1:2], EPS, None, ALU.add).then_inc(s_ve2, 1)

            def final_norm(j):
                dve.wait_ge(s_pw, j.n + 1)
                nc.vector.tensor_scalar(res[:, j.s, :], res[:, j.s, :], mv2[:, j.s, 0:1], rs2[:, j.s:j.s + 1],
                                        ALU.subtract, ALU.mult).then_inc(s_fin, 1)

            def step(tile):
                j = tile(0)
                if not j.const or j.n + 1 < NSL:
                    copy_hidden(tile(1))
                add_expert(j)
                if not j.const or j.n >= 2:
                    final_norm(tile(-2))
                stats2(j)
                variance2(j)

            copy_hidden(Tile(0, 0))
            sorted_tiles(dve, step)
            final_norm(Tile(0, NSL - 2))
            final_norm(Tile(0, NSL - 1))

        @block.gpsimd
        def _(pool):
            nc.gpsimd.memset(ident[:, :], 0.0).then_inc(s_id, 1)
            pool.wait_ge(s_id, 1)
            nc.gpsimd.affine_select(out=ident[:, :], in_=ident[:, :], compare_op=ALU.not_equal, fill=1.0, base=0,
                                    pattern=[[-1, P]], channel_multiplier=1).then_inc(s_id, 1)
            nc.gpsimd.memset(half_neg[:, :], -0.5).then_inc(s_rows, 1)
            nc.gpsimd.memset(rows[:, :], 0.0).then_inc(s_rows, 1)
            for i in range(3):
                pool.wait_ge(s_rows, i + 2)
                nc.gpsimd.affine_select(out=rows[:, :], in_=rows[:, :], compare_op=ALU.not_equal, fill=1.0,
                                        base=-2 * NS * i, pattern=[[-1, 2 * NS]],
                                        channel_multiplier=1).then_inc(s_rows, 1)

            nc.gpsimd.memset(zero[:, :], 0.0).then_inc(s_zc, 1)
            pool.wait_ge(s_zc, 1)
            nc.gpsimd.memset(zero[:, DM + 1:DM + 2], float(NTOK)).then_inc(s_zs, 1)
            nc.gpsimd.iota(iot[:, :, :], pattern=[[0, NT], [-1, NE]], base=NE, channel_multiplier=0).then_inc(s_iot, 1)
            nc.gpsimd.memset(trif[:, :], 1.0).then_inc(s_iot, 1)
            pool.wait_ge(s_iot, 2)
            nc.gpsimd.affine_select(out=trif[:, :], in_=trif[:, :], compare_op=ALU.is_gt, fill=0.0, base=0,
                                    pattern=[[1, P]], channel_multiplier=-1).then_inc(s_iot, 1)
            pool.wait_ge(s_iot, 3)
            nc.gpsimd.iota(tnoi[:, :, :], pattern=[[1, NSL], [0, NE]], base=0, channel_multiplier=0).then_inc(s_iot, 1)
            nc.gpsimd.iota(toki[:, :], pattern=[[P, NT]], base=0, channel_multiplier=1).then_inc(s_iot, 1)
            pool.wait_ge(s_iot, 5)

            def times_c(b, s):
                n = b.unit(s)
                pool.wait_ge(s_h, NH * (n + 1))
                pool.wait_ge(s_C[s % NB4], 16 * (NS // NB4 * b.n + s // NB4 + 1))
                wait(pool, s_y, NH * (n - NB4 + 1))
                nc.gpsimd.tensor_tensor(hc[:, s % NB4, :, :], hs[:, s % NB4, :, :],
                                        csb[:, s % NB4, :].unsqueeze(1).to_broadcast([P, NH, L]),
                                        ALU.mult).then_inc(s_hc, 1)

            def gate(b):
                pool.wait_ge(s_y2, 2 * (b.n + 1))
                pool.wait_ge(s_sz, b.n + 1)
                wait(pool, s_o, b.n)
                nc.gpsimd.tensor_tensor(yg[:, :, :], y2[:, :, :], sz[:, b.par, :, :], ALU.mult).then_inc(s_yg, 1)

            def norm(b):
                wait(pool, s_x1, TT * b.n)
                pool.wait_ge(s_ve, 2 * b.n + 2)
                nc.gpsimd.tensor_tensor(rstd[:, :], vare[:, :], half_neg[:, :], ALU.pow).then_inc(s_rstd, 1)

            def body(b):
                post = not b.first
                for s in range(NS):
                    times_c(b, s)
                    if s == 3 and post:
                        gate(b.step(-1))
                    if s == 13 and post:
                        norm(b.step(-1))

            def last_body(b):
                for s in range(NS):
                    times_c(b, s)
                    if s == 3:
                        gate(b.step(-1))
                    if s == 11:
                        norm(b.step(-1))
                gate(b)
                norm(b)

            sequences(pool, body, last_body)

            pool.wait_ge(s_slot, 1)
            pool.wait_ge(s_wt, 1)
            pool.wait_ge(s_tok, 1)
            pool.wait_ge(s_zf, 16)
            pool.wait_ge(s_x1, NT)
            for t in range(NT):
                nc.gpsimd.indirect_dma_start(xs_d, bass.IndirectOffsetOnAxis(ap=slot[:, t:t + 1], axis=0),
                                             x1[:, t, :], None).then_inc(s_sc, 16)

            def scatter(n):
                pool.wait_ge(s_fin, n + 1)
                pool.wait_ge(s_num, n + 1)
                nc.gpsimd.indirect_dma_start(out, bass.IndirectOffsetOnAxis(ap=num[:, n % STAGE:n % STAGE + 1], axis=0),
                                             res[:, n % STAGE, :], None, bounds_check=NTOK - 1,
                                             oob_is_err=False).then_inc(s_out[n % STAGE], 16)

            for n in range(NSL):
                if n >= 2:
                    scatter(n - 2)
                pool.wait_ge(s_ve2, n + 1)
                wait(pool, s_fin, n - STAGE + 1)
                nc.gpsimd.tensor_tensor(rs2[:, n % STAGE:n % STAGE + 1], ve2[:, n % STAGE:n % STAGE + 1],
                                        half_neg[:, 0:1], ALU.pow).then_inc(s_pw, 1)
            scatter(NSL - 2)
            scatter(NSL - 1)
            for k in range(STAGE):
                pool.wait_ge(s_out[k], 16 * NSL // STAGE)


def kernel(**inputs):
    import numpy as np
    import concourse.bacc as bacc
    from concourse.bass_utils import run_bass_kernel_spmd

    nc = bacc.Bacc("TRN2", target_bir_lowering=False, num_devices=1)
    w = {k[3:]: np.asarray(v) for k, v in inputs.items()}
    halves = lambda a: np.ascontiguousarray(a.reshape(NH, P, -1).transpose(1, 0, 2))
    x = w["attn_x"].reshape(B * TT, P, DM)
    arrays = {
        "x": np.ascontiguousarray(x.transpose(1, 0, 2)),
        "xT": np.ascontiguousarray(w["attn_x"].transpose(2, 0, 1)),
        "winN": halves(w["attn_W_in"][:DI]),
        "winzT": np.ascontiguousarray(w["attn_W_in"][DI:].T),
        "conv_w": halves(w["attn_conv_w"]),
        "conv_b": np.ascontiguousarray(halves(w["attn_conv_b"])[:, :, 0]),
        "wxT": halves(np.ascontiguousarray(w["attn_W_xproj"].T)),
        "w_dt": np.ascontiguousarray(halves(w["attn_W_dt"])[:, :, 0]),
        "b_dt": np.ascontiguousarray(halves(w["attn_b_dt"])[:, :, 0]),
        "a_log": halves(w["attn_A_log"]),
        "d_skip": np.ascontiguousarray(halves(w["attn_D"])[:, :, 0]),
        "woutT": halves(np.ascontiguousarray(w["attn_W_out"].T)),
        "wr": np.ascontiguousarray(w["ffn_Wr"]),
        "w1": np.ascontiguousarray(w["ffn_W1"].transpose(1, 0, 2)),
        "w2": np.ascontiguousarray(w["ffn_W2"].reshape(NE, HC, P, DM).transpose(2, 0, 1, 3)),
    }
    args = [nc.dram_tensor(f"in_{k}", v.shape, mybir.dt.from_np(v.dtype), kind="ExternalInput").ap()
            for k, v in arrays.items()]
    out = nc.dram_tensor("out_dram", (NTOK, DM), F32, kind="ExternalOutput").ap()
    build(nc, *args, out)
    r = run_bass_kernel_spmd(nc, [{f"in_{k}": v for k, v in arrays.items()}], core_ids=[0])
    return r.results[0]["out_dram"].reshape(B, L, DM)
```

```python
import concourse.bass as bass
from concourse import mybir
from contextlib import ExitStack

F32 = mybir.dt.float32
BF16 = mybir.dt.bfloat16
ALU = mybir.AluOpType
ACT = mybir.ActivationFunctionType

P = 128
B, L, DM = 8, 512, 128
DI, NS, KC = 256, 16, 4
NH = DI // P
TT = L // P
NT = B * TT
EPS = 1e-5
NE, HID = 8, 512
HC = HID // P
RING = 8
NSL = NT + NE - 1
RINGS = -(-NSL // RING)
YLAG = 5
BLEAD = 2
PE_CONV0 = 11
PE_CONV1 = 0
PE_DT = 4
PE_BC = 5
PE_OUT = 10
PE_Z0 = 7
PE_Z1 = 10
ACT_Z1 = 11
ACT_CONV0 = 15
ACT_CONV1 = 5
ACT_SILUZ = 5
ACT_DT = 8
ACT_EXP = 8
ACT_BC = 8
ACT_SQ = 9
ACT_SQ3 = 10
ACT_MID = 12
ACT_NORM = 3
ACT_Z0 = 11
DVE_GATE = 3
DVE_LOG = 7
DVE_DELTA = 11
DVE_REST = 8
DVE_LOW = 11
DVE_RES = 11
DVE_STAT = 12
DVE_SHIFT = 15
POOL_NORM = 12
POOL_U = 11
LATE = 1
TURN = 24
LAST_CHOOSE = 6
LAST_RANK = 7
LAST_OUT = 7
LAST_RES = 8
LAST_STAT = 8
LAST_SHIFT = 10
LAST_NORM = 8
STAGE = 4
XW = DM + 2
NTOK = NT * P
GT = 4
NG = NT // GT
PARTS = ((0, (B - 2) * TT), ((B - 2) * TT, NT))
EG = PARTS[0][1] // GT

LOG_PQ = [(1.0093576036046876, 1.1060657414085027), (-0.08225355201896584, 3.257478545131043),
          (-1.42473938465796, 2.7021118179052617), (-2.321691391327299, 0.43240818485899907)]
LOG_C = 0.005232626352594947


class Batch:

    def __init__(self, pair, base):
        self.pair, self.base = pair, base
        self.n = 2 * pair + base
        self.turn = pair + base // 2
        self.par = base % 2
        self.first = isinstance(pair, int) and self.n == 0
        self.late = LATE if self.first else 0
        self.before_last = isinstance(pair, int) and self.n == B - 2
        self.has_two_before = not (isinstance(pair, int) and self.n < 2)
        self.has_two_more = not (isinstance(pair, int) and self.n > B - 3)

    def step(self, d):
        return Batch(self.pair, self.base + d)

    def unit(self, s):
        return self.n * NS + s


class Tile:

    def __init__(self, ring, base):
        self.n = RING * ring + base
        self.const = isinstance(self.n, int)
        self.k, self.turn = base % RING, ring + base // RING
        self.s = base % STAGE
        self.sturn = RING // STAGE * ring + base // STAGE


def wait(eng, sem, value):
    if isinstance(value, int) and value <= 0:
        return
    eng.wait_ge(sem, value)


def build(nc, x, xT, winN, winzT, conv_w, conv_b, wxT, w_dt, b_dt, a_log, d_skip, woutT, wr, w1, w2, out):
    ctx = ExitStack()
    with ctx:
        def sb(name, shape, dt=F32):
            return ctx.enter_context(nc.sbuf_tensor(name, shape, dt))

        def pb(name, shape, dt=F32):
            return ctx.enter_context(nc.psum_tensor(name, shape, dt))

        def sem(name):
            return ctx.enter_context(nc.semaphore(name))

        win_nat = sb("win_nat", [P, NH, DM])
        winz = sb("winz", [P, DI])
        cw = sb("cw", [P, NH, KC])
        cb = sb("cb", [P, NH])
        wx = sb("wx", [P, NH, 1 + 2 * NS])
        wdt = sb("wdt", [P, NH])
        bdt = sb("bdt", [P, NH])
        alog = sb("alog", [P, NH, NS])
        A = sb("A", [P, NH, NS])
        dsk = sb("dsk", [P, NH])
        wout = sb("wout", [P, NH, DM])
        ident = sb("ident", [P, P])
        rest = sb("rest", [96, L])
        mid = sb("mid", [96, L], BF16)
        diagd = sb("diagd", [P, NH, P])
        diagw = sb("diagw", [P, NH, KC, P])
        wconv = sb("wconv", [P, NH, KC, P])
        wbc = sb("wbc", [P, NH, 3, 2 * NS])
        wdtb = sb("wdtb", [P, NH, P])
        pick = sb("pick", [96, NS, P], BF16)
        rows = sb("rows", [P, 2 * NS])
        logp = sb("logp", [P, len(LOG_PQ)])
        one_silu = sb("one_silu", [P, 1])
        half_neg = sb("half_neg", [P, TT])
        xtok = sb("xtok", [P, 2, TT, DM])
        cx = sb("cx", [P, NH, L])
        xc = sb("xc", [P, 2, NH, L])
        zraw = sb("zraw", [P, NH, L])
        sz = sb("sz", [P, 2, NH, L])
        relu = sb("relu", [P, NH, L])
        ex = sb("ex", [P, NH, L])
        sq = sb("sq", [P, 4, NH, L])
        delta = sb("delta", [P, 2, NH, L])
        u = sb("u", [P, 2, NH, L])
        parts = sb("parts", [96, 2, L], BF16)
        yg = sb("yg", [P, NH, L])
        rs = sb("rs", [P, TT, DM])
        st = sb("st", [P, TT, 6])
        mv = sb("mv", [P, TT, 2])
        vare = sb("vare", [P, TT])
        shifts = sb("shifts", [P, TT])
        rstd = sb("rstd", [P, TT])
        NB4 = 4
        da = sb("da", [P, NB4, NH, L])
        hs = sb("hs", [P, NB4, NH, L])
        hc = sb("hc", [P, NB4, NH, L])
        crow = sb("crow", [2 * NS, 2, L])
        csb = sb("csb", [P, NB4, L])
        x1 = sb("x1", [P, NT, XW])

        w1_sb = hs[:, :, :, :].rearrange("p b h t -> p (b h t)")
        w2_sb = hc[:, :, :, :].rearrange("p b h t -> p (b h t)")
        w1_tile = da[:, 0:2, :, :].rearrange("p b h t -> p (b h) t")
        hidT = da[:, 2:4, :, :].rearrange("p b h t -> p (b h) t")
        room = sq[:, :, :, :].rearrange("p a h t -> p (a h t)")
        rows_at, turned_at, res_at = 0, RING * XW, RING * XW + STAGE * P
        xs_sb = room[:, rows_at:turned_at].rearrange("p (i c) -> p i c", c=XW)
        xsT = room[:, turned_at:res_at].rearrange("p (i c) -> p i c", c=P)
        res = room[:, res_at:res_at + STAGE * DM].rearrange("p (i c) -> p i c", c=DM)
        xflat = x1[:, :, :].rearrange("p t c -> p (t c)")
        xTs = x1[:, :, :].rearrange("p (b t) c -> p b (t c)", b=B)
        XS = TT * XW
        wr_sb = sb("wr_sb", [P, NE])
        zero = sb("zero", [P, XW])
        tri = sb("tri", [P, P], BF16)
        ones = sb("ones", [P, P], BF16)
        x1T = sb("x1T", [P, 2, GT * P])
        key8 = sb("key8", [P, NT, NE])
        lgt = sb("lgt", [P, NT, NE])
        m1 = sb("m1", [P, NT])
        m2 = sb("m2", [P, NT])
        kmax = sb("kmax", [P, NT])
        key = sb("key", [P, NT, NE])
        hot = sb("hot", [P, NT, NE])
        hotb = [sb(f"hotb{i}", [P, NE, b - a], BF16) for i, (a, b) in enumerate(PARTS)]
        restl = sb("restl", [P, NT, NE])
        carry = [sb(f"carry{i}", [P, NE, b - a]) for i, (a, b) in enumerate(PARTS)]
        upto = [sb(f"upto{i}", [P, NE, b - a]) for i, (a, b) in enumerate(PARTS)]
        pos = [sb(f"pos{i}", [P, NE, b - a]) for i, (a, b) in enumerate(PARTS)]
        cnti = sb("cnti", [P, NE], mybir.dt.int32)
        tiles = sb("tiles", [P, NE])
        ends = sb("ends", [P, 2, NE])
        first_rows = sb("first_rows", [P, NE])
        room_rows = sb("room_rows", [P, NE])
        after = sb("after", [P, NE])
        jump = sb("jump", [P, NE])
        over = sb("over", [P, NE, PARTS[1][1] - PARTS[1][0]])
        start = sb("start", [P, NE])
        slotf = sb("slotf", [P, NT])
        slot = sb("slot", [P, NT], mybir.dt.uint32)
        tno = sb("tno", [1, NSL, 2 * NE])
        past = sb("past", [1, NSL, 2 * NE])
        share = sb("share", [1, NSL, 2 * NE])
        expf = sb("expf", [1, NSL])
        exps = sb("exps", [1, NSL], mybir.dt.int32)
        wtop = sb("wtop", [P, NT])
        st2 = sb("st2", [P, STAGE, 6])
        mv2 = sb("mv2", [P, STAGE, 2])
        ve2 = sb("ve2", [P, STAGE])
        rs2 = sb("rs2", [P, STAGE])
        num = sb("num", [P, STAGE], mybir.dt.uint32)
        toki = sb("toki", [P, NT], mybir.dt.int32)
        ones_f = sb("ones_f", [P, NE])
        trif = sb("trif", [P, P])
        iot = sb("iot", [P, NT, NE], mybir.dt.int32)
        tnoi = sb("tnoi", [1, NSL, 2 * NE], mybir.dt.int32)
        c_d = nc.dram_tensor("C_rows", (2, NS, L), F32, kind="Internal").ap()
        xs_d = nc.dram_tensor("sorted_tokens", (RINGS * RING * P, XW), F32, kind="Internal").ap()

        BU = [pb(f"BU{i}", [P, NH, L]) for i in range(2)]
        CB = pb("CB", [P, L])
        b_bank = lambda s: BU[s % NB4 // 2][:, s % 2, :]
        Y = pb("Y", [P, NH, L])
        PJ = pb("PJ", [P, L])

        s_wc = sem("conv_weights_in")
        s_w = sem("weights_in")
        s_id = sem("ident_made")
        s_pick = sem("pick_made")
        s_shift = sem("shifts_ready")
        s_rows = sem("rows_made")
        s_diag = sem("diag_made")
        s_prep = sem("dve_prep")
        s_wcp = sem("wconv_product")
        s_wcc = sem("wconv_copied")
        s_A = sem("A_made")
        s_xT = [sem(f"xT_in{i}") for i in range(2)]
        s_xt = [sem(f"xtok_in{i}") for i in range(2)]
        s_conv = sem("conv_ready")
        s_cx = sem("conv_copied")
        s_xc = sem("xconv_ready")
        s_dt = sem("dt_ready")
        s_dtu = sem("dt_read")
        s_e = sem("exp_small_ready")
        s_sq = sem("squares_ready")
        s_lg = sem("log_steps")
        s_dl = sem("delta_ready")
        s_u = sem("u_ready")
        s_bc = sem("bc_ready")
        s_hi = sem("bc_high")
        s_rest = sem("bc_rest")
        s_mid = sem("bc_mid")
        s_lo = sem("bc_low")
        s_z = sem("z_ready")
        s_zr = sem("z_copied")
        s_sz = sem("silu_z_ready")
        s_B = sem("B_spread")
        s_cr = sem("C_rows_ready")
        s_cd = sem("C_rows_in_dram")
        s_C = [sem(f"C_spread{i}") for i in range(NB4)]
        s_a = sem("decay_ready")
        s_ub = sem("ub_ready")
        s_h = sem("h_ready")
        s_hc = sem("hc_ready")
        s_y = sem("y_summed")
        s_yg = sem("y_gated")
        s_o = sem("out_ready")
        s_oa = sem("residual_added")
        s_st = sem("stats")
        s_mv = sem("mean_var")
        s_ve = sem("variance_eps_ready")
        s_rstd = sem("rstd_ready")
        s_x1 = sem("x1_ready")
        s_out = [sem(f"stored{i}") for i in range(STAGE)]
        s_we = sem("expert_weights_in")
        s_zc = sem("zero_cleared")
        s_zs = sem("zero_made")
        s_zf = sem("sorted_tokens_cleared")
        s_carry = sem("carry_ones")
        s_lgt = sem("logits_copied")
        s_tok = sem("numbers_in_rows")
        s_iot = sem("index_patterns")
        s_tri = sem("route_constants")
        s_xTp = sem("x1_transposed")
        s_xTc = sem("x1_transpose_copied")
        s_lo8 = sem("logits_ready")
        s_rt = sem("routing_steps")
        s_hot = sem("hot_ready")
        s_rank = sem("ranks_ready")
        s_slot = sem("slots_ready")
        s_dd = sem("second_minus_first_ready")
        s_ed = sem("exp_difference_ready")
        s_wt = sem("weights_ready")
        s_sc = sem("tokens_sorted")
        s_xs = [sem(f"sorted_tile_in{i}") for i in range(RING)]
        s_tx = sem("sorted_tile_transposed")
        s_txc = sem("sorted_tile_copied")
        s_m1 = sem("hidden_ready")
        s_ge = sem("gelu_ready")
        s_wt1 = sem("w1_of_tile_copied")
        s_m2 = sem("result_ready")
        s_r2 = sem("residual2_added")
        s_st2 = sem("stats2")
        s_num = sem("token_numbers")
        s_mv2 = sem("mean_var2")
        s_ve2 = sem("variance2_eps")
        s_pw = sem("rstd2_ready")
        s_fin = sem("final_ready")

        block = ctx.enter_context(nc.Block())

        def sequences(eng, body, last):
            body(Batch(0, 0))
            body(Batch(0, 1))
            with eng.Fori(1, B // 2 - 1) as pair:
                body(Batch(pair, 0))
                body(Batch(pair, 1))
            body(Batch(0, B - 2))
            last(Batch(0, B - 1))

        def sorted_tiles(eng, step):
            for i in range(RING):
                step(lambda d, i=i: Tile(0, i + d))
            with eng.Fori(1, RINGS - 1) as ring:
                for i in range(RING):
                    step(lambda d, i=i: Tile(ring, i + d))
            for i in range(NSL - RING * (RINGS - 1)):
                step(lambda d, i=i: Tile(RINGS - 1, i + d))

        @block.sync
        def _(sp):
            for dst, src in ((cw[:, :, :], conv_w), (win_nat[:, :, :], winN)):
                sp.dma_start(dst, src).then_inc(s_wc, 16)
            sp.dma_start(xTs[:, 0, KC - 1:KC - 1 + L], xT[:, 0, :]).then_inc(s_xT[0], 16)
            for dst, src in ((cb[:, :], conv_b), (wx[:, :, :], wxT), (wdt[:, :], w_dt), (bdt[:, :], b_dt),
                             (alog[:, :, :], a_log), (winz[:, :], winzT), (dsk[:, :], d_skip),
                             (wout[:, :, :], woutT), (wr_sb[:, :], wr)):
                sp.dma_start(dst, src).then_inc(s_w, 16)

            sp.dma_start(xTs[:, 1:, KC - 1:KC - 1 + L], xT[:, 1:, :]).then_inc(s_xT[1], 16)
            sp.wait_ge(s_zs, 1)
            sp.dma_start(xs_d.rearrange("(j p) c -> p j c", p=P),
                         zero[:, :].unsqueeze(1).to_broadcast([P, RINGS * RING, XW])).then_inc(s_zf, 16)

            def load_tokens(b):
                sp.dma_start(xtok[:, b.par, :, :], x[:, bass.ds(b.n * TT, TT), :]).then_inc(s_xt[b.par], 16)

            def c_out(b):
                sp.wait_ge(s_cr, b.n + 1)
                sp.dma_start(c_d[b.par], crow[NS:2 * NS, b.par, :]).then_inc(s_cd, 16)

            def spread_c(b, s):
                if s == 0:
                    sp.wait_ge(s_cd, 16 * (b.n + 1))
                if s % 2 == 1:
                    wait(sp, s_hc, b.unit(s) - NB4 + 2)
                sp.dma_start(csb[:, s % NB4, :],
                             c_d[b.par, s:s + 1, :].to_broadcast([P, L])).then_inc(s_C[s % NB4], 16)

            load_tokens(Batch(0, 0))
            c_out(Batch(0, 0))

            def body(b):
                for s in range(NS):
                    if s == 12 and not b.first:
                        sp.wait_ge(s_oa, b.n)
                    spread_c(b, s)
                    if s == 12:
                        load_tokens(b.step(1))
                    if s == 14:
                        c_out(b.step(1))

            def last_body(b):
                for s in range(NS):
                    spread_c(b, s)

            sequences(sp, body, last_body)
            sp.wait_ge(s_hc, B * NS)
            sp.dma_start(w1_sb.rearrange("p (e h) -> p e h", e=NE), w1).then_inc(s_we, 16)
            sp.wait_ge(s_y, B * NS * NH)
            sp.dma_start(w2_sb.rearrange("p (e k c) -> p e k c", e=NE, k=HC), w2).then_inc(s_we, 16)

            def load_tile(j):
                wait(sp, s_r2, j.n - RING + 1)
                wait(sp, s_num, j.n - RING + 1)
                sp.dma_start(xs_sb[:, j.k, :], xs_d[bass.ds(j.n * P, P), :]).then_inc(s_xs[j.k], 16)

            sp.wait_ge(s_sc, 16 * NT)
            for j in range(RING):
                load_tile(Tile(0, j))

            def step(tile):
                j = tile(RING)
                if not j.const or j.n < NSL:
                    load_tile(j)

            sorted_tiles(sp, step)
            for j in range(NSL, RINGS * RING):
                sp.wait_ge(s_xs[j % RING], 16 * RINGS)

        @block.tensor
        def _(pe):
            pe.wait_ge(s_wc, 32)
            for h in range(NH):
                pe.wait_ge(s_diag, (h + 1) * KC)
                for k in range(KC):
                    last = nc.tensor.matmul((PJ, CB)[h][:, k * P:(k + 1) * P], win_nat[:, h, :], diagw[:, h, k, :],
                                            start=True, stop=True)
                last.then_inc(s_wcp, 1)
            pe.wait_ge(s_prep, 1)

            def conv(b, h, taps=range(KC), bank=PJ):
                if 0 in taps:
                    if b.first:
                        pe.wait_ge(s_wcc, h + 1)
                    if h == 0:
                        if b.first:
                            pe.wait_ge(s_xT[0], 16)
                        elif isinstance(b.n, int) and b.n == 1:
                            pe.wait_ge(s_xT[1], 16)
                        wait(pe, s_zr, 2 * b.n)
                    elif not b.first:
                        pe.wait_ge(s_cx, 2 * b.n + 1)
                for k in taps:
                    last = nc.tensor.matmul(bank[:, :], wconv[:, h, k, :], xflat[:, bass.ds(b.n * XS + k, L)],
                                            start=(k == 0), stop=(k == KC - 1))
                if KC - 1 in taps:
                    last.then_inc(s_conv, 1)

            def dt(b):
                pe.wait_ge(s_xc, b.n + 1)
                for h in range(NH):
                    last = nc.tensor.matmul(PJ[:, :], wdtb[:, h, :], xc[:, b.par, h, :],
                                            start=(h == 0), stop=(h == NH - 1))
                last.then_inc(s_dt, 1)

            def bc(b):
                pe.wait_ge(s_xc, b.n + 1)
                wait(pe, s_rest, b.n)
                wait(pe, s_cr, b.n)
                wait(pe, s_oa, b.n - 2)
                for h in range(NH):
                    last = nc.tensor.matmul(CB[0:96, :], wbc[:, h, :, :].rearrange("p a s -> p (a s)"),
                                            xc[:, b.par, h, :], start=(h == 0), stop=(h == NH - 1))
                last.then_inc(s_bc, 1)

            def z(b, h):
                if h == 0:
                    pe.wait_ge(s_dtu, 4 * (b.n + 1))
                else:
                    pe.wait_ge(s_zr, 2 * b.n + 1)
                nc.tensor.matmul(PJ[:, :], winz[:, h * P:(h + 1) * P], xflat[:, bass.ds(b.n * XS + KC - 1, L)],
                                 start=True, stop=True).then_inc(s_z, 1)

            def out_proj(b, bank, tiles=range(TT)):
                if 0 in tiles:
                    pe.wait_ge(s_yg, b.n + 1)
                for j in tiles:
                    for h in range(NH):
                        last = nc.tensor.matmul(bank[:, j * P:(j + 1) * P], yg[:, h, j * P:(j + 1) * P],
                                                wout[:, h, :], start=(h == 0), stop=(h == NH - 1))
                if TT - 1 in tiles:
                    last.then_inc(s_o, 1)

            def spread_b(b, s):
                if s == 0:
                    pe.wait_ge(s_lo, b.n + 1)
                wait(pe, s_ub, b.unit(s) - NB4 + 1)
                nc.tensor.matmul(b_bank(s), pick[:, s, :], parts[:, b.par, :],
                                 start=True, stop=True).then_inc(s_B, 1)

            def y_sum(b, s, h):
                if s == 0:
                    wait(pe, s_yg, b.n)
                    nc.tensor.matmul(Y[:, h, :], diagd[:, h, :], xc[:, b.par, h, :], start=True, stop=False)
                pe.wait_ge(s_hc, b.unit(s) + 1)
                nc.tensor.matmul(Y[:, h, :], ident[:, :], hc[:, s % NB4, h, :],
                                 start=False, stop=(s == NS - 1)).then_inc(s_y, 1)

            first = Batch(0, 0)
            conv(first, 0)
            conv(first, 1, bank=BU[0][:, 0, :])
            pe.wait_ge(s_prep, 3)
            pe.wait_ge(s_w, 144)
            dt(first)
            bc(first)
            pe.wait_ge(s_prep, 5)
            z(first, 0)
            pe.wait_ge(s_pick, 1)
            for s in range(BLEAD):
                spread_b(first, s)

            def half_slot(b, s, h, more):
                if h == 0 and s + BLEAD < NS:
                    spread_b(b, s + BLEAD)
                elif h == 0 and more:
                    spread_b(b.step(1), s + BLEAD - NS)
                if s >= YLAG:
                    y_sum(b, s - YLAG, h)
                elif not b.first:
                    y_sum(b.step(-1), s - YLAG + NS, h)

            def early_routing(step):
                g, stage = divmod(step, 3)
                if 0 <= g < EG and stage == 0:
                    if g == 0:
                        pe.wait_ge(s_zr, 2 * B)
                    turn_tokens(g, PJ)
                if 0 <= g < EG and stage == 2:
                    if g == 0:
                        pe.wait_ge(s_oa, B - 2)
                    logits(g)

            def body(b):
                nb = b.step(1)
                for s in range(NS):
                    for h in range(NH):
                        half_slot(b, s, h, True)
                        if b.before_last:
                            early_routing(2 * s + h - TURN)
                        k = s - b.late
                        if b.first and s == 0 and h == 1:
                            z(b, 1)
                        if b.first and s == 1:
                            conv(nb, 0, [2 * h, 2 * h + 1])
                        if k - b.late in (PE_CONV1, PE_CONV1 + 1):
                            conv(nb, 1, [2 * (k - b.late - PE_CONV1) + h])
                        if k in (PE_CONV0, PE_CONV0 + 1) and b.has_two_more:
                            conv(b.step(2), 0, [2 * (k - PE_CONV0) + h])
                        if k == PE_DT and h == 1:
                            dt(nb)
                        if k == PE_BC and h == 1:
                            bc(nb)
                        if s in (PE_OUT, PE_OUT + 1) and not b.first:
                            if s == PE_OUT and h == 0:
                                pe.wait_ge(s_rest, b.n + 2)
                                pe.wait_ge(s_cr, b.n + 2)
                            out_proj(b.step(-1), CB, [2 * (s - PE_OUT) + h])
                        if k == PE_Z0 and h == 1:
                            z(nb, 0)
                        if k == PE_Z1 and h == 1:
                            z(nb, 1)

            def last_body(b):
                for s in range(NS):
                    for h in range(NH):
                        half_slot(b, s, h, False)
                        if s in (LAST_OUT, LAST_OUT + 1):
                            if s == LAST_OUT and h == 0:
                                pe.wait_ge(s_lgt, 1)
                            out_proj(b.step(-1), CB, [2 * (s - LAST_OUT) + h])
                        early_routing(2 * (NS + s) + h - TURN)
                        if s == LAST_RANK and h == 1:
                            ranks(0, PJ)
                for s in range(NS - YLAG, NS):
                    for h in range(NH):
                        y_sum(b, s, h)
                pe.wait_ge(s_ub, B * NS)
                pe.wait_ge(s_oa, B - 1)
                turn_tokens(EG, BU[0][:, 0, :])
                pe.wait_ge(s_slot, 1)
                out_proj(b, PJ)
                logits(EG)

            def turn_tokens(g, bank):
                pe.wait_ge(s_x1, GT * (g + 1))
                wait(pe, s_xTc, g)
                for i in range(GT):
                    last = nc.tensor.transpose(bank[:, i * P:(i + 1) * P], x1[:, g * GT + i, 0:DM], ident[:, :])
                last.then_inc(s_xTp, 1)

            def logits(g):
                pe.wait_ge(s_xTc, g + 1)
                for i in range(GT):
                    t = g * GT + i
                    last = nc.tensor.matmul(CB[:, t * NE:(t + 1) * NE], x1T[:, g % 2, i * P:(i + 1) * P],
                                            wr_sb[:, :], start=True, stop=True)
                last.then_inc(s_lo8, 1)

            def ranks(part, bank):
                pe.wait_ge(s_tri, 7)
                pe.wait_ge(s_hot, part + 1)
                hot_all = hotb[part][:, :, :].rearrange("p e i -> p (e i)")
                n = NE * (PARTS[part][1] - PARTS[part][0])
                nc.tensor.matmul(bank[:, 0:n], tri[:, :], hot_all, start=True, stop=True).then_inc(s_rank, 1)
                nc.tensor.matmul(bank[:, n:2 * n], ones[:, :], hot_all, start=True, stop=True).then_inc(s_rank, 1)

            sequences(pe, body, last_body)

            turn_tokens(NG - 1, BU[0][:, 1, :])
            logits(NG - 1)
            pe.wait_ge(s_yg, B)
            ranks(1, Y[:, 0, :])

            def tile_in(j):
                pe.wait_ge(s_xs[j.k], 16 * (j.turn + 1))
                wait(pe, s_txc, j.n)
                nc.tensor.transpose(CB[:, 0:P], xs_sb[:, j.k, 0:DM], ident[:, :]).then_inc(s_tx, 1)

            def expert(j):
                return pe.value_load(exps[0:1, bass.ds(j.n, 1)], min_val=0, max_val=(NE - 1) * HID)

            def up(j):
                pe.wait_ge(s_wt1, j.n + 1)
                pe.wait_ge(s_txc, j.n + 1)
                wait(pe, s_ge, j.n - 1)
                for c in range(HC):
                    last = nc.tensor.matmul(BU[0][:, j.k % 2, c * P:(c + 1) * P], w1_tile[:, j.s, c * P:(c + 1) * P],
                                            xsT[:, j.s, :], start=True, stop=True)
                last.then_inc(s_m1, 1)

            def down(j):
                e = expert(j)
                pe.wait_ge(s_ge, j.n + 1)
                wait(pe, s_r2, j.n - 1)
                for c in range(HC):
                    last = nc.tensor.matmul(Y[:, j.k % 2, 0:DM], hidT[:, j.s, c * P:(c + 1) * P],
                                            w2_sb[:, c * DM:][:, bass.ds(e, DM)],
                                            start=(c == 0), stop=(c == HC - 1))
                last.then_inc(s_m2, 1)

            def step(tile):
                j = tile(0)
                if not j.const or j.n + 2 < NSL:
                    tile_in(tile(2))
                if not j.const or j.n + 1 < NSL:
                    up(tile(1))
                if not j.const or j.n >= 1:
                    down(tile(-1))

            pe.wait_ge(s_slot, 3)
            tile_in(Tile(0, 0))
            tile_in(Tile(0, 1))
            pe.wait_ge(s_we, 32)
            up(Tile(0, 0))
            sorted_tiles(pe, step)
            down(Tile(0, NSL - 1))

        @block.scalar
        def _(act):
            for h in range(NH):
                act.wait_ge(s_wcp, h + 1)
                nc.scalar.copy(wconv[:, h, :, :].rearrange("p k d -> p (k d)"), (PJ, CB)[h][:, :]).then_inc(s_wcc, 1)
            act.wait_ge(s_id, 2)
            nc.scalar.activation(one_silu[:, :], ident[:, 0:1], ACT.Silu)
            act.wait_ge(s_w, 144)
            act.wait_ge(s_prep, 5)

            def copy_conv(b, h, bank=PJ):
                act.wait_ge(s_conv, 2 * b.n + h + 1)
                nc.scalar.activation(cx[:, h, :], bank[:, :], ACT.Identity, bias=cb[:, h:h + 1]).then_inc(s_cx, 1)

            def silu_x(b):
                act.wait_ge(s_cx, 2 * b.n + 2)
                wait(act, s_y, ((b.n - 2) * NS + 1) * NH)
                nc.scalar.activation(xc[:, b.par, :, :], cx[:, :, :], ACT.Silu).then_inc(s_xc, 1)

            def silu_z(b):
                act.wait_ge(s_zr, 2 * b.n + 2)
                wait(act, s_yg, b.n - 1)
                nc.scalar.activation(sz[:, b.par, :, :], zraw[:, :, :], ACT.Silu).then_inc(s_sz, 1)

            def softplus_in(b):
                act.wait_ge(s_dt, b.n + 1)
                wait(act, s_dl, b.n)
                for h in range(NH):
                    nc.scalar.activation(ex[:, h, :], PJ[:, :], ACT.Abs, scale=wdt[:, h:h + 1],
                                         bias=bdt[:, h:h + 1]).then_inc(s_dtu, 1)
                    nc.scalar.activation(relu[:, h, :], PJ[:, :], ACT.Relu, scale=wdt[:, h:h + 1],
                                         bias=bdt[:, h:h + 1]).then_inc(s_dtu, 1)

            def softplus_exp(b):
                act.wait_ge(s_dtu, 4 * (b.n + 1))
                nc.scalar.activation(ex[:, :, :], ex[:, :, :], ACT.Exp, scale=-1.0).then_inc(s_e, 1)

            def square(b, i):
                act.wait_ge(s_e, b.n + 1)
                nc.scalar.activation(sq[:, i, :, :], ex[:, :, :], ACT.Square, bias=logp[:, i:i + 1]).then_inc(s_sq, 1)

            def bc_high(b):
                act.wait_ge(s_bc, b.n + 1)
                wait(act, s_B, (b.n - 1) * NS)
                nc.scalar.copy(parts[:, b.par, :], CB[0:96, :]).then_inc(s_hi, 1)

            def bc_mid(b):
                act.wait_ge(s_rest, b.n + 1)
                nc.scalar.copy(parts[32:64, b.par, :], rest[32:64, :]).then_inc(s_mid, 1)
                wait(act, s_lo, b.n)
                nc.scalar.copy(mid[64:96, :], rest[64:96, :]).then_inc(s_mid, 1)

            def copy_z(b, h):
                act.wait_ge(s_z, 2 * b.n + h + 1)
                wait(act, s_sz, b.n)
                nc.scalar.copy(zraw[:, h, :], PJ[:, :]).then_inc(s_zr, 1)

            def decay(b, s):
                n = b.unit(s)
                if s == 0:
                    act.wait_ge(s_dl, b.n + 1)
                wait(act, s_h, n - NB4 + 1)
                for h in range(NH):
                    nc.scalar.activation(da[:, s % NB4, h, 1:], delta[:, b.par, h, 1:], ACT.Exp,
                                         scale=A[:, h, s:s + 1]).then_inc(s_a, 1)

            def c_rows(b):
                act.wait_ge(s_bc, b.n + 1)
                for i in range(NB4):
                    wait(act, s_C[i], 16 * (NS // NB4) * (b.n - 1))
                nc.scalar.copy(crow[:, b.par, :], CB[0:2 * NS, :]).then_inc(s_cr, 1)

            def normalize(b):
                act.wait_ge(s_shift, b.n + 1)
                for j in range(TT):
                    nc.scalar.activation(x1[:, bass.ds(b.n * TT + j, 1), 0:DM].rearrange("p a c -> p (a c)"),
                                         rs[:, j, :], ACT.Identity, bias=shifts[:, j:j + 1],
                                         scale=rstd[:, j:j + 1]).then_inc(s_x1, 1)

            first = Batch(0, 0)
            copy_conv(first, 0)
            copy_conv(first, 1, BU[0][:, 0, :])
            silu_x(first)
            nc.scalar.activation(A[:, :, :], alog[:, :, :], ACT.Exp).then_inc(s_A, 1)
            act.wait_ge(s_A, 1)
            nc.scalar.mul(A[:, :, :], A[:, :, :], -1.0).then_inc(s_A, 1)
            act.wait_ge(s_A, 2)
            softplus_in(first)
            softplus_exp(first)
            square(first, 0)
            bc_high(first)
            c_rows(first)
            square(first, 1)
            square(first, 2)
            bc_mid(first)
            square(first, 3)
            copy_z(first, 0)

            def body(b):
                nb = b.step(1)
                for s in range(NS):
                    decay(b, s)
                    k = s - b.late
                    if k == ACT_CONV1:
                        copy_conv(nb, 1)
                        silu_x(nb)
                    if k == ACT_SILUZ:
                        silu_z(b)
                    if k == ACT_DT:
                        softplus_in(nb)
                    if k == ACT_EXP:
                        softplus_exp(nb)
                        square(nb, 0)
                    if k == ACT_BC:
                        bc_high(nb)
                        c_rows(nb)
                    if k == ACT_SQ:
                        square(nb, 1)
                        square(nb, 2)
                    if k == ACT_SQ3:
                        square(nb, 3)
                    if k == ACT_MID:
                        bc_mid(nb)
                    if s == ACT_NORM and b.has_two_before:
                        normalize(b.step(-2))
                    if b.first and s == 2:
                        copy_z(b, 1)
                    if b.first and s == 4:
                        copy_conv(nb, 0)
                    if k == ACT_Z0:
                        copy_z(nb, 0)
                    if k == ACT_Z1:
                        copy_z(nb, 1)
                    if b.before_last:
                        early_copies(s)
                    if s == min(ACT_CONV0 + b.late, NS - 1) and b.has_two_more:
                        copy_conv(b.step(2), 0)

            def early_copies(unit):
                for g in range(EG):
                    if unit == (TURN + 3 * g) // 2 + 2:
                        copy_turned(g, PJ)

            def copy_turned(g, bank):
                act.wait_ge(s_xTp, g + 1)
                wait(act, s_lo8, g - 1)
                nc.scalar.copy(x1T[:, g % 2, :], bank[:, :]).then_inc(s_xTc, 1)

            def exp_difference(part):
                a, e = PARTS[part]
                act.wait_ge(s_dd, part + 1)
                nc.scalar.activation(wtop[:, a:e], m2[:, a:e], ACT.Exp).then_inc(s_ed, 1)

            def last_body(b):
                for s in range(NS):
                    decay(b, s)
                    if s == ACT_SILUZ:
                        silu_z(b)
                    if s == ACT_NORM:
                        normalize(b.step(-2))
                    early_copies(NS + s)
                    if s == NS - 1:
                        exp_difference(0)
                normalize(b.step(-1))

            sequences(act, body, last_body)

            copy_turned(EG, BU[0][:, 0, :])
            normalize(Batch(0, B - 1))
            copy_turned(NG - 1, BU[0][:, 1, :])
            exp_difference(1)

            def copy_tile(j):
                act.wait_ge(s_tx, j.n + 1)
                wait(act, s_m1, j.n - STAGE + 1)
                nc.scalar.copy(xsT[:, j.s, :], CB[:, 0:P]).then_inc(s_txc, 1)

            def gelu(j):
                act.wait_ge(s_m1, j.n + 1)
                wait(act, s_m2, j.n - STAGE + 1)
                nc.scalar.activation(hidT[:, j.s, :], BU[0][:, j.k % 2, :], ACT.Gelu).then_inc(s_ge, 1)

            def step(tile):
                j = tile(0)
                if not j.const or j.n + 2 < NSL:
                    copy_tile(tile(2))
                if not j.const or j.n + 1 < NSL:
                    gelu(tile(1))

            copy_tile(Tile(0, 0))
            copy_tile(Tile(0, 1))
            gelu(Tile(0, 0))
            sorted_tiles(act, step)

        @block.vector
        def _(dve):
            nc.vector.memset(xTs[:, :, 0:KC - 1], 0.0).then_inc(s_prep, 1)
            dve.wait_ge(s_id, 2)
            dve.wait_ge(s_wc, 32)
            for h in range(NH):
                for k in range(KC):
                    nc.vector.tensor_scalar(diagw[:, h, k, :], ident[:, :], cw[:, h, k:k + 1], None,
                                            ALU.mult).then_inc(s_diag, 1)
            for i, (p, _) in enumerate(LOG_PQ):
                nc.vector.memset(logp[:, i:i + 1], p)
            nc.vector.memset(da[:, :, :, 0:1], 0.0)
            dve.wait_ge(s_w, 144)
            for i in range(3):
                last = nc.vector.tensor_copy(wbc[:, :, i, :], wx[:, :, 1:])
            last.then_inc(s_prep, 1)
            nc.vector.tensor_copy(wdtb[:, :, :], wx[:, :, 0:1].to_broadcast([P, NH, P])).then_inc(s_prep, 1)
            for h in range(NH):
                nc.vector.tensor_scalar(diagd[:, h, :], ident[:, :], dsk[:, h:h + 1], None, ALU.mult).then_inc(s_prep, 1)

            dve.wait_ge(s_rows, 5)
            nc.vector.tensor_copy(pick[:, :, :], rows[0:96, 0:NS].unsqueeze(2).to_broadcast([96, NS, P])).then_inc(s_pick, 1)

            dve.wait_ge(s_iot, 5)
            nc.vector.memset(ones[:, :], 1.0).then_inc(s_tri, 1)
            nc.vector.tensor_copy(tri[:, :], trif[:, :]).then_inc(s_tri, 1)
            nc.vector.memset(share[:, :, :], 1.0).then_inc(s_carry, 1)
            nc.vector.tensor_copy(key8[:, :, :], iot[:, :, :]).then_inc(s_tri, 1)
            nc.vector.tensor_copy(tno[:, :, :], tnoi[:, :, :]).then_inc(s_tri, 1)
            nc.vector.memset(ones_f[:, :], 1.0).then_inc(s_tri, 1)
            for part in range(2):
                nc.vector.memset(carry[part][:, :, :], 1.0).then_inc(s_carry, 1)
            dve.wait_ge(s_carry, 3)
            for part in range(2):
                last = nc.vector.memset(carry[part][:, :, 0:1], 0.0)
            last.then_inc(s_tri, 1)
            nc.vector.memset(share[:, :, NE - 1:NE], float(1 - NE)).then_inc(s_tri, 1)

            def bc_rest(b):
                dve.wait_ge(s_hi, b.n + 1)
                dve.wait_ge(s_cr, b.n + 1)
                wait(dve, s_mid, 2 * b.n)
                nc.vector.tensor_tensor(rest[:, :], CB[0:96, :], parts[:, b.par, :], ALU.subtract).then_inc(s_rest, 1)

            def bc_low(b):
                dve.wait_ge(s_mid, 2 * b.n + 2)
                nc.vector.tensor_tensor(parts[64:96, b.par, :], rest[64:96, :], mid[64:96, :],
                                        ALU.subtract).then_inc(s_lo, 1)

            def log_step(b, i):
                dve.wait_ge(s_sq, 4 * b.n + i + 1)
                if i:
                    dve.wait_ge(s_lg, 4 * b.n + i)
                before = ex[:, :, :] if i == 0 else sq[:, i - 1, :, :]
                nc.vector.scalar_tensor_tensor(sq[:, i, :, :], sq[:, i, :, :], LOG_PQ[i][1], before,
                                               ALU.add, ALU.mult).then_inc(s_lg, 1)

            def make_delta(b):
                dve.wait_ge(s_lg, 4 * b.n + 4)
                wait(dve, s_a, (b.n - 1) * NS * NH)
                nc.vector.scalar_tensor_tensor(delta[:, b.par, :, :], sq[:, 3, :, :], LOG_C, relu[:, :, :],
                                               ALU.mult, ALU.add).then_inc(s_dl, 1)

            def make_ub(b, s):
                n = b.unit(s)
                if s == 0:
                    dve.wait_ge(s_u, b.n + 1)
                dve.wait_ge(s_B, n + 1)
                wait(dve, s_hc, n - NB4 + 1)
                nc.vector.tensor_tensor(hs[:, s % NB4, :, :], b_bank(s).unsqueeze(1).to_broadcast([P, NH, L]),
                                        u[:, b.par, :, :], ALU.mult).then_inc(s_ub, 1)

            def scan(b, s):
                n = b.unit(s)
                dve.wait_ge(s_ub, n + 1)
                dve.wait_ge(s_a, NH * (n + 1))
                flat = hs[:, s % NB4, :, :].rearrange("p h t -> p (h t)")
                nc.vector.tensor_tensor_scan(flat, da[:, s % NB4, :, :].rearrange("p h t -> p (h t)"), flat,
                                             0.0, ALU.mult, ALU.add).then_inc(s_h, 1)

            def unit(b, s, more):
                if s + 1 < NS:
                    make_ub(b, s + 1)
                elif more:
                    make_ub(b.step(1), 0)
                scan(b, s)

            def gate(b):
                dve.wait_ge(s_y, (b.n + 1) * NS * NH)
                dve.wait_ge(s_sz, b.n + 1)
                wait(dve, s_o, b.n)
                nc.vector.tensor_tensor(yg[:, :, :], Y[:, :, :], sz[:, b.par, :, :], ALU.mult).then_inc(s_yg, 1)

            def add_residual(b, bank=CB):
                dve.wait_ge(s_o, b.n + 1)
                dve.wait_ge(s_xt[b.par], 16 * (b.turn + 1))
                wait(dve, s_x1, TT * b.n)
                nc.vector.tensor_tensor(rs[:, :, :].rearrange("p j c -> p (j c)"), bank[:, :],
                                        xtok[:, b.par, :, :].rearrange("p j c -> p (j c)"),
                                        ALU.add).then_inc(s_oa, 1)

            def stats(b):
                dve.wait_ge(s_oa, b.n + 1)
                for j in range(TT):
                    nc.vector.bn_stats(st[:, j, :], rs[:, j, :]).then_inc(s_st, 1)

            def mean_var(b):
                wait(dve, s_rstd, b.n)
                dve.wait_ge(s_st, TT * (b.n + 1))
                nc.vector.memset(vare[:, :], EPS).then_inc(s_ve, 1)
                for j in range(TT):
                    nc.vector.bn_aggr(mv[:, j, :], st[:, j, :]).then_inc(s_mv, 1)
                dve.wait_ge(s_mv, TT * (b.n + 1))
                dve.wait_ge(s_ve, 2 * b.n + 1)
                nc.vector.tensor_tensor(vare[:, :], mv[:, :, 1], vare[:, :], ALU.add).then_inc(s_ve, 1)

            def shift(b):
                dve.wait_ge(s_rstd, b.n + 1)
                wait(dve, s_x1, TT * b.n)
                nc.vector.scalar_tensor_tensor(shifts[:, :], mv[:, :, 0], -1.0, rstd[:, :],
                                               ALU.mult, ALU.mult).then_inc(s_shift, 1)

            first = Batch(0, 0)
            log_step(first, 0)
            bc_rest(first)
            log_step(first, 1)
            log_step(first, 2)
            bc_low(first)
            log_step(first, 3)
            make_delta(first)
            dve.wait_ge(s_dl, 1)
            nc.vector.tensor_tensor(u[:, 0, :, :], delta[:, 0, :, :], xc[:, 0, :, :], ALU.mult).then_inc(s_u, 1)
            make_ub(first, 0)

            def body(b):
                nb = b.step(1)
                post = not b.first
                for s in range(NS):
                    unit(b, s, True)
                    k = s - b.late
                    if s == DVE_GATE and post:
                        gate(b.step(-1))
                    if DVE_LOG <= k < DVE_LOG + 4:
                        log_step(nb, k - DVE_LOG)
                    if k == DVE_REST:
                        bc_rest(nb)
                    if k == DVE_LOW:
                        bc_low(nb)
                    if k == DVE_DELTA:
                        make_delta(nb)
                    if s == DVE_RES and post:
                        add_residual(b.step(-1))
                    if s == DVE_STAT and post:
                        stats(b.step(-1))
                        mean_var(b.step(-1))
                    if s == DVE_SHIFT and post:
                        shift(b.step(-1))

            steps = [0]

            def link(ins):
                steps[0] += 1
                ins.then_inc(s_rt, 1)
                dve.wait_ge(s_rt, steps[0])

            AX = mybir.AxisListType.X

            def token_numbers():
                dve.wait_ge(s_z, 2 * B)
                nc.vector.tensor_copy(x1[:, :, DM + 1:DM + 2], toki[:, :].unsqueeze(2)).then_inc(s_tok, 1)

            def choose(part):
                a, e = PARTS[part]
                n = e - a

                def per_tile(v):
                    return v.unsqueeze(2).to_broadcast([P, n, NE])

                lg, k, ht = lgt[:, a:e, :], key[:, a:e, :], hot[:, a:e, :]
                dve.wait_ge(s_lo8, e // GT)
                dve.wait_ge(s_tri, 7)
                nc.vector.tensor_copy(lg.rearrange("p t e -> p (t e)"), CB[:, a * NE:e * NE]).then_inc(s_lgt, 1)
                dve.wait_ge(s_lgt, part + 1)
                link(nc.vector.tensor_reduce(m1[:, a:e], lg, axis=AX, op=ALU.max))
                link(nc.vector.tensor_tensor(k, lg, per_tile(m1[:, a:e]), ALU.is_equal))
                link(nc.vector.tensor_tensor(k, k, key8[:, a:e, :], ALU.mult))
                link(nc.vector.tensor_reduce(kmax[:, a:e], k, axis=AX, op=ALU.max))
                link(nc.vector.tensor_tensor(ht, k, per_tile(kmax[:, a:e]), ALU.is_equal))
                nc.vector.tensor_copy(hotb[part][:, :, :].rearrange("p e t -> p t e"), ht).then_inc(s_hot, 1)
                link(nc.vector.scalar_tensor_tensor(restl[:, a:e, :], ht, -3.0e38, lg, ALU.mult, ALU.add))
                link(nc.vector.tensor_reduce(m2[:, a:e], restl[:, a:e, :], axis=AX, op=ALU.max))
                nc.vector.tensor_tensor(m2[:, a:e], m2[:, a:e], m1[:, a:e], ALU.subtract).then_inc(s_dd, 1)

            def weigh(part):
                a, e = PARTS[part]
                dve.wait_ge(s_ed, part + 1)
                link(nc.vector.tensor_scalar(wtop[:, a:e], wtop[:, a:e], 1.0, None, ALU.add))
                nc.vector.reciprocal(x1[:, a:e, DM:DM + 1], wtop[:, a:e].unsqueeze(2)).then_inc(s_wt, 1)

            def count(part, bank):
                n = NE * (PARTS[part][1] - PARTS[part][0])
                totals = bank[:, n:2 * n]
                dve.wait_ge(s_rank, 2 * (part + 1))
                link(nc.vector.tensor_tensor_scan(upto[part][:, :, :].rearrange("p e t -> p (e t)"),
                                                  carry[part][:, :, :].rearrange("p e t -> p (e t)"), totals,
                                                  0.0, ALU.mult, ALU.add))
                link(nc.vector.tensor_tensor(pos[part][:, :, :], upto[part][:, :, :],
                                             totals.rearrange("p (e t) -> p e t", e=NE), ALU.subtract))
                link(nc.vector.tensor_tensor(pos[part][:, :, :], pos[part][:, :, :],
                                             bank[:, 0:n].rearrange("p (e t) -> p e t", e=NE), ALU.add))

            def to_slots(part):
                a, e = PARTS[part]
                link(nc.vector.tensor_tensor(pos[part][:, :, :], pos[part][:, :, :],
                                             hot[:, a:e, :].rearrange("p t e -> p e t"), ALU.mult))
                link(nc.vector.tensor_reduce(slotf[:, a:e], pos[part][:, :, :].rearrange("p e t -> p t e"),
                                             axis=AX, op=ALU.add))
                nc.vector.tensor_copy(slot[:, a:e], slotf[:, a:e]).then_inc(s_slot, 1)

            def full_tiles():
                link(nc.vector.tensor_single_scalar(cnti[:, :], cnti[:, :], 7, ALU.logical_shift_right))

            def place_early():
                n = PARTS[0][1] - PARTS[0][0]
                count(0, PJ)
                link(nc.vector.tensor_scalar(cnti[:, :], upto[0][:, :, n - 1], float(P - 1), None, ALU.add))
                full_tiles()
                link(nc.vector.tensor_copy(tiles[:, :], cnti[:, :]))
                link(nc.vector.tensor_tensor_scan(ends[:, 0, :], ones_f[:, :], tiles[:, :], 0.0, ALU.mult, ALU.add))
                link(nc.vector.tensor_tensor(start[:, :], ends[:, 0, :], tiles[:, :], ALU.subtract))
                link(nc.vector.tensor_scalar(first_rows[:, :], start[:, :], float(P), None, ALU.mult))
                link(nc.vector.tensor_scalar(room_rows[:, :], tiles[:, :], float(P), None, ALU.mult))
                link(nc.vector.tensor_tensor(pos[0][:, :, :], pos[0][:, :, :],
                                             first_rows[:, :].unsqueeze(2).to_broadcast([P, NE, n]), ALU.add))
                to_slots(0)

            def place_late():
                n = PARTS[1][1] - PARTS[1][0]
                last_early = upto[0][:, :, PARTS[0][1] - PARTS[0][0] - 1]

                def per_expert(v):
                    return v.unsqueeze(2).to_broadcast([P, NE, n])

                count(1, Y[:, 0, :])
                link(nc.vector.scalar_tensor_tensor(cnti[:, :], upto[1][:, :, n - 1], float(P - 1), last_early,
                                                    ALU.add, ALU.add))
                full_tiles()
                link(nc.vector.tensor_tensor(after[:, :], cnti[:, :], tiles[:, :], ALU.subtract))
                link(nc.vector.tensor_tensor_scan(ends[:, 1, :], ones_f[:, :], after[:, :], 0.0, ALU.mult, ALU.add))
                link(nc.vector.tensor_scalar(ends[:, 1, :], ends[:, 1, :], ends[:, 0, NE - 1:NE], None, ALU.add))
                link(nc.vector.tensor_tensor(jump[:, :], ends[:, 1, :], after[:, :], ALU.subtract))
                link(nc.vector.tensor_tensor(jump[:, :], jump[:, :], ends[:, 0, :], ALU.subtract))
                link(nc.vector.tensor_tensor(pos[1][:, :, :], pos[1][:, :, :], per_expert(last_early), ALU.add))
                link(nc.vector.tensor_tensor(over[:, :, :], pos[1][:, :, :], per_expert(room_rows[:, :]), ALU.is_ge))
                link(nc.vector.tensor_tensor(pos[1][:, :, :], pos[1][:, :, :], per_expert(first_rows[:, :]), ALU.add))
                link(nc.vector.scalar_tensor_tensor(over[:, :, :], over[:, :, :], float(P), per_expert(jump[:, :]),
                                                    ALU.mult, ALU.mult))
                link(nc.vector.tensor_tensor(pos[1][:, :, :], pos[1][:, :, :], over[:, :, :], ALU.add))
                to_slots(1)

            def expert_of_tiles():
                link(nc.vector.tensor_tensor(past[:, :, :], tno[:, :, :],
                                             ends[0:1, :, :].rearrange("p a e -> p (a e)").unsqueeze(1)
                                             .to_broadcast([1, NSL, 2 * NE]), ALU.is_ge))
                link(nc.vector.tensor_tensor(past[:, :, :], past[:, :, :], share[:, :, :], ALU.mult))
                link(nc.vector.tensor_reduce(expf[:, :], past[:, :, :], axis=AX, op=ALU.add))
                nc.vector.tensor_scalar(exps[:, :], expf[:, :], float(NE - 1), float(HID), ALU.min,
                                        ALU.mult).then_inc(s_slot, 1)

            def last_body(b):
                for s in range(NS):
                    unit(b, s, False)
                    if s == 1:
                        token_numbers()
                    if s == LAST_CHOOSE:
                        choose(0)
                    if s == NS - 1:
                        weigh(0)
                    if s == DVE_GATE:
                        gate(b.step(-1))
                    if s == LAST_RES:
                        add_residual(b.step(-1))
                    if s == LAST_STAT:
                        stats(b.step(-1))
                        mean_var(b.step(-1))
                    if s == LAST_SHIFT:
                        shift(b.step(-1))
                place_early()
                gate(b)
                add_residual(b, PJ)
                stats(b)
                mean_var(b)
                shift(b)

            sequences(dve, body, last_body)

            choose(1)
            place_late()
            weigh(1)
            expert_of_tiles()

            def expert(j):
                return dve.value_load(exps[0:1, bass.ds(j.n, 1)], min_val=0, max_val=(NE - 1) * HID)

            def copy_w1(j, e):
                nc.vector.tensor_copy(w1_tile[:, j.s, :], w1_sb[:, bass.ds(e, HID)]).then_inc(s_wt1, 1)

            def add_expert(j):
                dve.wait_ge(s_m2, j.n + 1)
                wait(dve, s_out[j.s], 16 * j.sturn)
                nc.vector.scalar_tensor_tensor(res[:, j.s, :], Y[:, j.k % 2, 0:DM], xs_sb[:, j.k, DM:DM + 1],
                                               xs_sb[:, j.k, 0:DM], ALU.mult, ALU.add).then_inc(s_r2, 1)

            def stats2(j):
                dve.wait_ge(s_r2, j.n + 1)
                nc.vector.bn_stats(st2[:, j.s, :], res[:, j.s, :]).then_inc(s_st2, 1)
                dve.wait_ge(s_st2, j.n + 1)
                nc.vector.tensor_copy(num[:, j.s:j.s + 1], xs_sb[:, j.k, DM + 1:DM + 2]).then_inc(s_num, 1)
                nc.vector.bn_aggr(mv2[:, j.s, :], st2[:, j.s, :]).then_inc(s_mv2, 1)

            def variance2(j):
                dve.wait_ge(s_mv2, j.n + 1)
                wait(dve, s_pw, j.n - STAGE + 1)
                nc.vector.tensor_scalar(ve2[:, j.s:j.s + 1], mv2[:, j.s, 1:2], EPS, None, ALU.add).then_inc(s_ve2, 1)

            def final_norm(j):
                dve.wait_ge(s_pw, j.n + 1)
                nc.vector.tensor_scalar(res[:, j.s, :], res[:, j.s, :], mv2[:, j.s, 0:1], rs2[:, j.s:j.s + 1],
                                        ALU.subtract, ALU.mult).then_inc(s_fin, 1)

            def step(tile):
                j = tile(0)
                copies = not j.const or j.n + STAGE < NSL
                e = expert(tile(STAGE)) if copies else None
                add_expert(j)
                if copies:
                    copy_w1(tile(STAGE), e)
                if not j.const or j.n >= 2:
                    final_norm(tile(-2))
                stats2(j)
                variance2(j)

            dve.wait_ge(s_slot, 3)
            dve.wait_ge(s_we, 32)
            for n in range(STAGE):
                copy_w1(Tile(0, n), expert(Tile(0, n)))
            sorted_tiles(dve, step)
            final_norm(Tile(0, NSL - 2))
            final_norm(Tile(0, NSL - 1))

        @block.gpsimd
        def _(pool):
            nc.gpsimd.memset(ident[:, :], 0.0).then_inc(s_id, 1)
            pool.wait_ge(s_id, 1)
            nc.gpsimd.affine_select(out=ident[:, :], in_=ident[:, :], compare_op=ALU.not_equal, fill=1.0, base=0,
                                    pattern=[[-1, P]], channel_multiplier=1).then_inc(s_id, 1)
            nc.gpsimd.memset(half_neg[:, :], -0.5).then_inc(s_rows, 1)
            nc.gpsimd.memset(rows[:, :], 0.0).then_inc(s_rows, 1)
            for i in range(3):
                pool.wait_ge(s_rows, i + 2)
                nc.gpsimd.affine_select(out=rows[:, :], in_=rows[:, :], compare_op=ALU.not_equal, fill=1.0,
                                        base=-2 * NS * i, pattern=[[-1, 2 * NS]],
                                        channel_multiplier=1).then_inc(s_rows, 1)

            nc.gpsimd.memset(zero[:, :], 0.0).then_inc(s_zc, 1)
            pool.wait_ge(s_zc, 1)
            nc.gpsimd.memset(zero[:, DM + 1:DM + 2], float(NTOK)).then_inc(s_zs, 1)
            nc.gpsimd.iota(iot[:, :, :], pattern=[[0, NT], [-1, NE]], base=NE, channel_multiplier=0).then_inc(s_iot, 1)
            nc.gpsimd.memset(trif[:, :], 1.0).then_inc(s_iot, 1)
            pool.wait_ge(s_iot, 2)
            nc.gpsimd.affine_select(out=trif[:, :], in_=trif[:, :], compare_op=ALU.is_gt, fill=0.0, base=0,
                                    pattern=[[1, P]], channel_multiplier=-1).then_inc(s_iot, 1)
            pool.wait_ge(s_iot, 3)
            nc.gpsimd.iota(tnoi[:, :, :], pattern=[[1, NSL], [0, 2 * NE]], base=0, channel_multiplier=0).then_inc(s_iot, 1)
            nc.gpsimd.iota(toki[:, :], pattern=[[P, NT]], base=0, channel_multiplier=1).then_inc(s_iot, 1)
            pool.wait_ge(s_iot, 5)

            def times_c(b, s):
                n = b.unit(s)
                pool.wait_ge(s_h, n + 1)
                pool.wait_ge(s_C[s % NB4], 16 * (NS // NB4 * b.n + s // NB4 + 1))
                wait(pool, s_y, NH * (n - NB4 + 1))
                nc.gpsimd.tensor_tensor(hc[:, s % NB4, :, :], hs[:, s % NB4, :, :],
                                        csb[:, s % NB4, :].unsqueeze(1).to_broadcast([P, NH, L]),
                                        ALU.mult).then_inc(s_hc, 1)

            def make_u(b):
                pool.wait_ge(s_dl, b.n + 1)
                wait(pool, s_ub, NS * (b.n - 1))
                nc.gpsimd.tensor_tensor(u[:, b.par, :, :], delta[:, b.par, :, :], xc[:, b.par, :, :],
                                        ALU.mult).then_inc(s_u, 1)

            def norm(b):
                wait(pool, s_x1, TT * b.n)
                pool.wait_ge(s_ve, 2 * b.n + 2)
                nc.gpsimd.tensor_tensor(rstd[:, :], vare[:, :], half_neg[:, :], ALU.pow).then_inc(s_rstd, 1)

            def body(b):
                post = not b.first
                for s in range(NS):
                    times_c(b, s)
                    if s - b.late == POOL_U:
                        make_u(b.step(1))
                    if s == POOL_NORM and post:
                        norm(b.step(-1))

            def last_body(b):
                for s in range(NS):
                    times_c(b, s)
                    if s == LAST_NORM:
                        norm(b.step(-1))
                pool.wait_ge(s_tok, 1)
                pool.wait_ge(s_zf, 16)
                pool.wait_ge(s_slot, 1)
                pool.wait_ge(s_wt, 1)
                pool.wait_ge(s_x1, PARTS[0][1])
                for t in range(*PARTS[0]):
                    if t == POOL_LAST_NORM:
                        norm(b)
                    rows_out(t)
                pool.wait_ge(s_slot, 2)
                pool.wait_ge(s_wt, 2)
                pool.wait_ge(s_x1, NT)
                for t in range(*PARTS[1]):
                    rows_out(t)


            def rows_out(t):
                nc.gpsimd.indirect_dma_start(xs_d, bass.IndirectOffsetOnAxis(ap=slot[:, t:t + 1], axis=0),
                                             x1[:, t, :], None).then_inc(s_sc, 16)

            POOL_LAST_NORM = 8
            sequences(pool, body, last_body)

            def scatter(n):
                pool.wait_ge(s_fin, n + 1)
                pool.wait_ge(s_num, n + 1)
                nc.gpsimd.indirect_dma_start(out, bass.IndirectOffsetOnAxis(ap=num[:, n % STAGE:n % STAGE + 1], axis=0),
                                             res[:, n % STAGE, :], None, bounds_check=NTOK - 1,
                                             oob_is_err=False).then_inc(s_out[n % STAGE], 16)

            for n in range(NSL):
                if n >= 2:
                    scatter(n - 2)
                pool.wait_ge(s_ve2, n + 1)
                wait(pool, s_fin, n - STAGE + 1)
                nc.gpsimd.tensor_tensor(rs2[:, n % STAGE:n % STAGE + 1], ve2[:, n % STAGE:n % STAGE + 1],
                                        half_neg[:, 0:1], ALU.pow).then_inc(s_pw, 1)
            scatter(NSL - 2)
            scatter(NSL - 1)
            for k in range(STAGE):
                pool.wait_ge(s_out[k], 16 * len(range(k, NSL, STAGE)))


def kernel(**inputs):
    import numpy as np
    import concourse.bacc as bacc
    from concourse.bass_utils import run_bass_kernel_spmd

    nc = bacc.Bacc("TRN2", target_bir_lowering=False, num_devices=1)
    w = {k[3:]: np.asarray(v) for k, v in inputs.items()}
    halves = lambda a: np.ascontiguousarray(a.reshape(NH, P, -1).transpose(1, 0, 2))
    x = w["attn_x"].reshape(B * TT, P, DM)
    arrays = {
        "x": np.ascontiguousarray(x.transpose(1, 0, 2)),
        "xT": np.ascontiguousarray(w["attn_x"].transpose(2, 0, 1)),
        "winN": halves(w["attn_W_in"][:DI]),
        "winzT": np.ascontiguousarray(w["attn_W_in"][DI:].T),
        "conv_w": halves(w["attn_conv_w"]),
        "conv_b": np.ascontiguousarray(halves(w["attn_conv_b"])[:, :, 0]),
        "wxT": halves(np.ascontiguousarray(w["attn_W_xproj"].T)),
        "w_dt": np.ascontiguousarray(halves(w["attn_W_dt"])[:, :, 0]),
        "b_dt": np.ascontiguousarray(halves(w["attn_b_dt"])[:, :, 0]),
        "a_log": halves(w["attn_A_log"]),
        "d_skip": np.ascontiguousarray(halves(w["attn_D"])[:, :, 0]),
        "woutT": halves(np.ascontiguousarray(w["attn_W_out"].T)),
        "wr": np.ascontiguousarray(w["ffn_Wr"]),
        "w1": np.ascontiguousarray(w["ffn_W1"].transpose(1, 0, 2)),
        "w2": np.ascontiguousarray(w["ffn_W2"].reshape(NE, HC, P, DM).transpose(2, 0, 1, 3)),
    }
    args = [nc.dram_tensor(f"in_{k}", v.shape, mybir.dt.from_np(v.dtype), kind="ExternalInput").ap()
            for k, v in arrays.items()]
    out = nc.dram_tensor("out_dram", (NTOK, DM), F32, kind="ExternalOutput").ap()
    build(nc, *args, out)
    r = run_bass_kernel_spmd(nc, [{f"in_{k}": v for k, v in arrays.items()}], core_ids=[0])
    return r.results[0]["out_dram"].reshape(B, L, DM)
```
